# Optimizing a Trainium2 kernel written in Bass

```python
import numpy as np
import jax
import jax.numpy as jnp

def _softmax(x, axis=-1):
    return jax.nn.softmax(x, axis=axis)

def _gelu(x):
    return jax.nn.gelu(x, approximate=True)

def _silu(x):
    return jax.nn.silu(x)

def _sigmoid(x):
    return jax.nn.sigmoid(x)

def _layernorm(x, axis=-1, eps=1e-05):
    m = jnp.mean(x, axis=axis, keepdims=True)
    v = jnp.var(x, axis=axis, keepdims=True)
    return (x - m) / jnp.sqrt(v + eps)

def _scatter_add(tgt, idx, src, axis=0):
    return tgt.at[idx].add(src)

def _segment_sum(src, seg, n):
    return jax.ops.segment_sum(src, seg, n)
kernel_name = 'mk_sandwich_d1_jaxref_r8_d37a5f'

def setup_inputs(seed: int=0):
    np.random.seed(seed)
    _w = jnp.asarray

    def _L0_attn_setup():
        import jax, jax.numpy as jnp
        import numpy as np
        B, T, C, H = (4, 256, 128, 16)
        INIT_STD = 0.02
        key = jax.random.key(seed)
        ks = jax.random.split(key, 9)
        x = jax.random.normal(ks[0], (B, T, C), dtype=jnp.float32)

        def dense(kw):
            return jax.random.normal(kw, (C, C), dtype=jnp.float32) * INIT_STD
        return {'x': x, 'Wq': dense(ks[1]), 'bq': jnp.zeros((C,), jnp.float32), 'Wk': dense(ks[2]), 'bk': jnp.zeros((C,), jnp.float32), 'Wv': dense(ks[3]), 'bv': jnp.zeros((C,), jnp.float32), 'Wo': dense(ks[4]), 'bo': jnp.zeros((C,), jnp.float32)}
    _L0_attn_in = _L0_attn_setup()

    def _L0_ffn_setup():
        import jax, jax.numpy as jnp
        import numpy as np
        DIM = 128
        DEPTH = 6
        HEADS = 16
        DIM_HEAD = 64
        WINDOW = 32
        INNER = HEADS * DIM_HEAD
        DIM_INNER = int(DIM * 4 * 2 / 3)
        QK_SCALE = 8.0

        def shift_tokens(t):
            a, s = jnp.split(t, 2, -1)
            s = jnp.pad(s, ((0, 0), (1, 0), (0, 0)))[:, :-1]
            return jnp.concatenate([a, s], -1)

        def l2norm(t):
            return t / jnp.maximum(jnp.linalg.norm(t, axis=-1, keepdims=True), 1e-12)

        def rotate_half(x):
            x1, x2 = jnp.split(x, 2, -1)
            return jnp.concatenate([-x2, x1], -1)

        def rotary_tables(n):
            half = jnp.arange(0, DIM_HEAD, 2, dtype=jnp.float32)
            inv_freq = 1.0 / 10000.0 ** (half / DIM_HEAD)
            t = jnp.arange(n, dtype=jnp.float32)
            freqs = t[:, None] * inv_freq[None, :]
            freqs = jnp.concatenate([freqs, freqs], -1)
            base_scale = (half + 0.4 * DIM_HEAD) / (1.4 * DIM_HEAD)
            power = (t - n // 2) / (WINDOW // 2)
            scale = base_scale[None, :] ** power[:, None]
            scale = jnp.concatenate([scale, scale], -1)
            return (freqs, scale)

        def local_attention(q, k, v):
            b, h, n, d = q.shape
            w = WINDOW
            nw = n // w
            bq = q.reshape(b, h, nw, w, d)
            bk = k.reshape(b, h, nw, w, d)
            bv = v.reshape(b, h, nw, w, d)

            def look(t):
                p = jnp.pad(t, ((0, 0), (0, 0), (1, 0), (0, 0), (0, 0)))
                return jnp.concatenate([p[:, :, :nw], p[:, :, 1:]], axis=3)
            bk2, bv2 = (look(bk), look(bv))
            seq = jnp.arange(n).reshape(nw, w)
            seq_p = jnp.pad(seq, ((1, 0), (0, 0)), constant_values=-1)
            jt = jnp.concatenate([seq_p[:nw], seq_p[1:]], axis=1)
            it = seq[:, :, None]
            jb = jt[:, None, :]
            mask = (it < jb) | (it > jb + w) | (jb == -1)
            sim = jnp.einsum('bhwie,bhwje->bhwij', bq, bk2) * QK_SCALE
            sim = jnp.where(mask, -jnp.finfo(sim.dtype).max, sim)
            attn = jax.nn.softmax(sim, -1)
            out = jnp.einsum('bhwij,bhwje->bhwie', attn, bv2)
            return out.reshape(b, h, n, d)

        def attn_layer(x, Wqkv, qs, ksc, Wo):
            b, n, _ = x.shape
            qkv = x @ Wqkv
            q, k, v = jnp.split(qkv, 3, -1)
            sh = lambda t: t.reshape(b, n, HEADS, DIM_HEAD).transpose(0, 2, 1, 3)
            q, k, v = (sh(q), sh(k), sh(v))
            q = l2norm(q) * qs
            k = l2norm(k) * ksc
            freqs, scale = rotary_tables(n)
            cos, sin = (jnp.cos(freqs), jnp.sin(freqs))
            q = q * cos * scale + rotate_half(q) * sin * scale
            inv = 1.0 / scale
            k = k * cos * inv + rotate_half(k) * sin * inv
            out = local_attention(q, k, v)
            out = out.transpose(0, 2, 1, 3).reshape(b, n, INNER)
            return out @ Wo

        def ffn_layer(x, g, bln, W1, b1, W2, b2):
            mu = x.mean(-1, keepdims=True)
            var = ((x - mu) ** 2).mean(-1, keepdims=True)
            xn = (x - mu) / jnp.sqrt(var + 1e-05) * g + bln
            hg = xn @ W1 + b1
            a, gate = jnp.split(hg, 2, -1)
            return a * jax.nn.gelu(gate, approximate=False) @ W2 + b2
        key = jax.random.key(seed)
        ks = jax.random.split(key, 8)
        B, N = (2, 256)
        init = lambda k, shape: jax.random.normal(k, shape, jnp.float32) * 0.02
        return {'x': jax.random.normal(ks[0], (B, N, DIM), jnp.float32), 'Wqkv': init(ks[1], (DEPTH, DIM, 3 * INNER)), 'q_scale': jnp.ones((DEPTH, DIM_HEAD), jnp.float32), 'k_scale': jnp.ones((DEPTH, DIM_HEAD), jnp.float32), 'Wo': init(ks[2], (DEPTH, INNER, DIM)), 'ln_g': jnp.ones((DEPTH, DIM), jnp.float32), 'ln_b': jnp.zeros((DEPTH, DIM), jnp.float32), 'W1': init(ks[3], (DEPTH, DIM, 2 * DIM_INNER)), 'b1': jnp.zeros((DEPTH, 2 * DIM_INNER), jnp.float32), 'W2': init(ks[4], (DEPTH, DIM_INNER, DIM)), 'b2': jnp.zeros((DEPTH, DIM), jnp.float32)}
    _L0_ffn_in = _L0_ffn_setup()
    _d = {'L0_attn_x': _L0_attn_in['x'], 'L0_attn_Wq': _L0_attn_in['Wq'], 'L0_attn_bq': _L0_attn_in['bq'], 'L0_attn_Wk': _L0_attn_in['Wk'], 'L0_attn_bk': _L0_attn_in['bk'], 'L0_attn_Wv': _L0_attn_in['Wv'], 'L0_attn_bv': _L0_attn_in['bv'], 'L0_attn_Wo': _L0_attn_in['Wo'], 'L0_attn_bo': _L0_attn_in['bo'], 'L0_ffn_Wqkv': _L0_ffn_in['Wqkv'], 'L0_ffn_q_scale': _L0_ffn_in['q_scale'], 'L0_ffn_k_scale': _L0_ffn_in['k_scale'], 'L0_ffn_Wo': _L0_ffn_in['Wo'], 'L0_ffn_ln_g': _L0_ffn_in['ln_g'], 'L0_ffn_ln_b': _L0_ffn_in['ln_b'], 'L0_ffn_W1': _L0_ffn_in['W1'], 'L0_ffn_b1': _L0_ffn_in['b1'], 'L0_ffn_W2': _L0_ffn_in['W2'], 'L0_ffn_b2': _L0_ffn_in['b2']}
    _x0 = _d['L0_attn_x']
    _d['L0_attn_x'] = jax.random.normal(jax.random.fold_in(jax.random.key(seed), 1), (1, 2048, 128), dtype=_x0.dtype)
    del _x0
    return _d

def reference(L0_attn_x, L0_attn_Wq, L0_attn_bq, L0_attn_Wk, L0_attn_bk, L0_attn_Wv, L0_attn_bv, L0_attn_Wo, L0_attn_bo, L0_ffn_Wqkv, L0_ffn_q_scale, L0_ffn_k_scale, L0_ffn_Wo, L0_ffn_ln_g, L0_ffn_ln_b, L0_ffn_W1, L0_ffn_b1, L0_ffn_W2, L0_ffn_b2):

    def _L0_attn_ref(x, Wq, bq, Wk, bk, Wv, bv, Wo, bo):
        import jax, jax.numpy as jnp
        import numpy as np
        B, T, C, H = (4, 256, 128, 16)
        INIT_STD = 0.02
        b, t, c = x.shape
        hd = c // H

        def split_heads(y):
            return jnp.transpose(y.reshape(b, t, H, hd), (0, 2, 1, 3))
        q = split_heads(x @ Wq + bq)
        k = split_heads(x @ Wk + bk)
        v = split_heads(x @ Wv + bv)
        scale = 1.0 / jnp.sqrt(jnp.float32(hd))
        att = jnp.einsum('bhqd,bhkd->bhqk', q, k) * scale
        mask = jnp.tril(jnp.ones((t, t), dtype=bool))[None, None]
        att = jnp.where(mask, att, jnp.float32(-jnp.inf))
        att = jax.nn.softmax(att, axis=-1)
        y = jnp.einsum('bhqk,bhkd->bhqd', att, v)
        y = jnp.transpose(y, (0, 2, 1, 3)).reshape(b, t, c)
        return y @ Wo + bo

    def _L0_ffn_ref(x, Wqkv, q_scale, k_scale, Wo, ln_g, ln_b, W1, b1, W2, b2):
        import jax, jax.numpy as jnp
        import numpy as np
        DIM = 128
        DEPTH = 6
        HEADS = 16
        DIM_HEAD = 64
        WINDOW = 32
        INNER = HEADS * DIM_HEAD
        DIM_INNER = int(DIM * 4 * 2 / 3)
        QK_SCALE = 8.0

        def shift_tokens(t):
            a, s = jnp.split(t, 2, -1)
            s = jnp.pad(s, ((0, 0), (1, 0), (0, 0)))[:, :-1]
            return jnp.concatenate([a, s], -1)

        def l2norm(t):
            return t / jnp.maximum(jnp.linalg.norm(t, axis=-1, keepdims=True), 1e-12)

        def rotate_half(x):
            x1, x2 = jnp.split(x, 2, -1)
            return jnp.concatenate([-x2, x1], -1)

        def rotary_tables(n):
            half = jnp.arange(0, DIM_HEAD, 2, dtype=jnp.float32)
            inv_freq = 1.0 / 10000.0 ** (half / DIM_HEAD)
            t = jnp.arange(n, dtype=jnp.float32)
            freqs = t[:, None] * inv_freq[None, :]
            freqs = jnp.concatenate([freqs, freqs], -1)
            base_scale = (half + 0.4 * DIM_HEAD) / (1.4 * DIM_HEAD)
            power = (t - n // 2) / (WINDOW // 2)
            scale = base_scale[None, :] ** power[:, None]
            scale = jnp.concatenate([scale, scale], -1)
            return (freqs, scale)

        def local_attention(q, k, v):
            b, h, n, d = q.shape
            w = WINDOW
            nw = n // w
            bq = q.reshape(b, h, nw, w, d)
            bk = k.reshape(b, h, nw, w, d)
            bv = v.reshape(b, h, nw, w, d)

            def look(t):
                p = jnp.pad(t, ((0, 0), (0, 0), (1, 0), (0, 0), (0, 0)))
                return jnp.concatenate([p[:, :, :nw], p[:, :, 1:]], axis=3)
            bk2, bv2 = (look(bk), look(bv))
            seq = jnp.arange(n).reshape(nw, w)
            seq_p = jnp.pad(seq, ((1, 0), (0, 0)), constant_values=-1)
            jt = jnp.concatenate([seq_p[:nw], seq_p[1:]], axis=1)
            it = seq[:, :, None]
            jb = jt[:, None, :]
            mask = (it < jb) | (it > jb + w) | (jb == -1)
            sim = jnp.einsum('bhwie,bhwje->bhwij', bq, bk2) * QK_SCALE
            sim = jnp.where(mask, -jnp.finfo(sim.dtype).max, sim)
            attn = jax.nn.softmax(sim, -1)
            out = jnp.einsum('bhwij,bhwje->bhwie', attn, bv2)
            return out.reshape(b, h, n, d)

        def attn_layer(x, Wqkv, qs, ksc, Wo):
            b, n, _ = x.shape
            qkv = x @ Wqkv
            q, k, v = jnp.split(qkv, 3, -1)
            sh = lambda t: t.reshape(b, n, HEADS, DIM_HEAD).transpose(0, 2, 1, 3)
            q, k, v = (sh(q), sh(k), sh(v))
            q = l2norm(q) * qs
            k = l2norm(k) * ksc
            freqs, scale = rotary_tables(n)
            cos, sin = (jnp.cos(freqs), jnp.sin(freqs))
            q = q * cos * scale + rotate_half(q) * sin * scale
            inv = 1.0 / scale
            k = k * cos * inv + rotate_half(k) * sin * inv
            out = local_attention(q, k, v)
            out = out.transpose(0, 2, 1, 3).reshape(b, n, INNER)
            return out @ Wo

        def ffn_layer(x, g, bln, W1, b1, W2, b2):
            mu = x.mean(-1, keepdims=True)
            var = ((x - mu) ** 2).mean(-1, keepdims=True)
            xn = (x - mu) / jnp.sqrt(var + 1e-05) * g + bln
            hg = xn @ W1 + b1
            a, gate = jnp.split(hg, 2, -1)
            return a * jax.nn.gelu(gate, approximate=False) @ W2 + b2
        for i in range(DEPTH):
            x = attn_layer(shift_tokens(x), Wqkv[i], q_scale[i], k_scale[i], Wo[i]) + x
            x = ffn_layer(shift_tokens(x), ln_g[i], ln_b[i], W1[i], b1[i], W2[i], b2[i]) + x
        return x
    x = L0_attn_x
    x = x + _layernorm(_L0_attn_ref(_layernorm(x, axis=-1), L0_attn_Wq, L0_attn_bq, L0_attn_Wk, L0_attn_bk, L0_attn_Wv, L0_attn_bv, L0_attn_Wo, L0_attn_bo), axis=-1)
    x = x + _layernorm(_L0_ffn_ref(_layernorm(x, axis=-1), L0_ffn_Wqkv, L0_ffn_q_scale, L0_ffn_k_scale, L0_ffn_Wo, L0_ffn_ln_g, L0_ffn_ln_b, L0_ffn_W1, L0_ffn_b1, L0_ffn_W2, L0_ffn_b2), axis=-1)
    return x

_drawn_inputs = setup_inputs


def setup_inputs(seed=0):
    import zlib

    import numpy as np

    out = dict(_drawn_inputs(seed))
    spreads = {'L0_attn_bq': (0.0, 0.8),
     'L0_attn_bk': (0.0, 2.0),
     'L0_attn_bv': (0.0, 0.1),
     'L0_attn_bo': (0.0, 0.1),
     'L0_ffn_q_scale': (1.0, 0.6),
     'L0_ffn_k_scale': (1.0, 0.6),
     'L0_ffn_ln_g': (1.0, 0.6),
     'L0_ffn_ln_b': (0.0, 0.8),
     'L0_ffn_b1': (0.0, 0.8),
     'L0_ffn_b2': (0.0, 0.375)}
    factors = {'L0_attn_Wq': 8.0, 'L0_attn_Wk': 8.0, 'L0_ffn_W1': 4.449, 'L0_ffn_W2': 4.352}
    for name, (base, spread) in spreads.items():
        noise = np.random.default_rng([zlib.crc32(name.encode()), seed]).standard_normal(out[name].shape)
        drawn = base * np.exp(spread * noise) if base else spread * noise
        out[name] = jnp.asarray(drawn.astype(out[name].dtype))
    for name, factor in factors.items():
        out[name] = (out[name] * factor).astype(out[name].dtype)
    return out
```

```python
from contextlib import ExitStack

import numpy as np
import concourse.bass as bass
from concourse import mybir

F32 = mybir.dt.float32
BF16 = mybir.dt.bfloat16
ALU = mybir.AluOpType
ACT = mybir.ActivationFunctionType
AX = mybir.AxisListType

P = 128
T, C = 2048, 128
NT = T // P
EPS = 1e-5
H1, D1 = 16, 8
HG, NHG = 4, 4
NPAIR = 9
ROWS = NPAIR * D1
QC = 512
NQC = T // QC
SCALE1 = 1.0 / float(np.sqrt(np.float32(D1)))
L, H, DH, W = 6, 16, 64, 32
INNER = H * DH
FF = int(C * 4 * 2 / 3)
WPT = P // W
NTILE = L * NT
QK_SCALE = 8.0
NEG = -3.0e38


def constants():
    half = np.arange(0, DH, 2, dtype=np.float64)
    freq = 1.0 / 10000.0 ** (half / DH)
    base = (half + 0.4 * DH) / (1.4 * DH)
    p = np.arange(P)[:, None]
    ang = np.concatenate([p * freq, p * freq], -1)
    grow = base ** (p / (W // 2))
    grow = np.concatenate([grow, grow], -1)
    sign = np.where(np.arange(DH) < DH // 2, -1.0, 1.0)
    rot = np.stack([np.cos(ang) * grow * QK_SCALE, sign * np.sin(ang) * grow * QK_SCALE,
                    np.cos(ang) / grow, sign * np.sin(ang) / grow], 1)
    c, s, g = np.cos(P * freq), np.sin(P * freq), base ** (P / (W // 2))
    back = np.zeros((P, P))
    n = DH // 2
    for h in (0, DH):
        for f in range(n):
            back[h + f, h + f] = c[f] * g[f]
            back[h + n + f, h + f] = s[f] * g[f]
            back[h + n + f, h + n + f] = c[f] * g[f]
            back[h + f, h + n + f] = -s[f] * g[f]
    centre = np.eye(P) - 1.0 / C
    a = np.arange(W)
    pattern = np.zeros((P, 2 * W))
    pattern[:W, :W] = np.where(a[None, :] < a[:, None], NEG, 0)
    pattern[W:2 * W, :W] = NEG
    pattern[:W, W:] = pattern[W:2 * W, W:] = np.where(a[None, :] > a[:, None], NEG, 0)
    select = np.zeros((P, NT, P))
    for m in range(P):
        select[m % W, :, m] = 1
    for m in range(W):
        select[m, 0, m], select[W + m, 0, m] = 0, 1
    carry = np.ones((P, NT))
    carry[:, 0] = 0
    r = np.arange(P)
    tri_q = np.where(r[None, :] > r[:, None], NEG, 0)
    tri_k = np.zeros((P, QC))
    tri_k[:, :QC - P] = NEG
    tri_k[:, QC - P:] = np.where(r[:, None] > r[None, :], NEG, 0)
    f = lambda x: np.ascontiguousarray(x, dtype=np.float32)
    b = lambda x: np.ascontiguousarray((f(x).view(np.uint32) >> 16).astype(np.uint16))
    return {
        "c_rot": f(rot), "c_back": f(back), "c_centre": f(centre), "c_pattern": b(pattern),
        "c_select": b(select), "c_carry": f(carry), "c_tri_q": b(tri_q), "c_tri_k": b(tri_k),
        "c_ident": f(np.eye(P)), "c_mean": f(np.full((P, P), 1.0 / C)),
        "c_zeros": b(np.zeros((3, HG * T))), "c_ones": b(np.ones((3, HG * T))),
    }


def schedule():
    steps = [(qc, kt) for qc in range(NQC) for kt in range(QC // P * (qc + 1))]
    pieces = [(h, t, c) for h in range(HG) for t in range(NT) for c in range(1 + (t >= NT // 2))]
    order, done = [], 0
    for s, (qc, kt) in enumerate(steps):
        order.append(("score", s))
        if s >= 1:
            order.append(("pv", s - 1))
        if s >= 2 and steps[s - 2][0] != steps[s - 1][0]:
            order.append(("out", steps[s - 2][0]))
            order[-1], order[-2] = order[-2], order[-1]
        want = len(pieces) * (s + 1) // len(steps)
        while done < want:
            order.append(("max", done))
            done += 1
    order += [("pv", len(steps) - 1), ("out", NQC - 1)]
    return steps, pieces, order


def build(nc, a, out):
    steps, pieces, order = schedule()
    NS = len(steps)
    NPC = len(pieces)
    nc.disable_value_cache = True
    with ExitStack() as ctx:
        def sb(name, shape, dt=F32):
            return ctx.enter_context(nc.sbuf_tensor(name, shape, dt))

        def sem(name):
            return ctx.enter_context(nc.semaphore(name))

        bank = ctx.enter_context(nc.psum_tensor("bank", [P, 8, 512], F32))

        qk_parts = nc.dram_tensor("qk_parts", (2, 3, P, T), BF16, kind="Internal").ap()
        max_parts = nc.dram_tensor("max_parts", (NHG, 3, HG * NT, P), BF16, kind="Internal").ap()

        x = sb("x", [P, NT, C])
        kept = sb("kept", [P, NT, C])
        ident = sb("ident", [P, P])
        identb = sb("identb", [P, P], BF16)
        stat = sb("stat", [P, 6, NT])
        wqk = sb("wqk", [P, 2, 2 * INNER])
        wv = sb("wv", [P, INNER])
        wo = sb("wo", [P, 2, 8, C])
        w1 = sb("w1", [P, 2, 2 * FF])
        w2 = sb("w2", [P, 2, 3, C])
        b1 = sb("b1", [P, 2, 2 * FF])
        b2 = sb("b2", [P, 2, C])
        ln_g = sb("ln_g", [P, L])
        ln_b = sb("ln_b", [P, L])
        rot = sb("rot", [P, 4, DH])
        qks = sb("qks", [P, 2, L, DH])
        table = sb("table", [P, L, 2, 2, DH])
        back = sb("back", [P, P])
        centre = sb("centre", [P, P])
        mean = sb("mean", [P, P])
        pattern = sb("pattern", [P, 2 * W], BF16)
        pattern8 = sb("pattern8", [P, 8, 2 * W], BF16)
        select = sb("select", [P, NT, P], BF16)
        carry = sb("carry", [P, NT])

        arena = sb("arena", [P, 26880])
        used = [0]

        def part(*shape, dt=F32):
            size = int(np.prod(shape)) // (2 if dt == BF16 else 1)
            v = arena[:, used[0]:used[0] + size]
            used[0] += size
            assert used[0] <= 26880, used
            if dt != F32:
                v = v.bitcast(dt)
            if len(shape) == 1:
                return v
            names = "abcdef"[:len(shape)]
            return v.rearrange(f"p ({' '.join(names)}) -> p {' '.join(names)}",
                               **{n: d for n, d in zip(names[1:], shape[1:])})

        qst = part(2, HG, T, dt=BF16)
        kst = part(2, HG, T, dt=BF16)
        ring = part(8, QC)
        _ = part(QC, 4)
        used[0] -= 4 * QC
        o_sb = part(QC)
        vaug = part(NT, H1, D1 + 1)
        vcur = part(NT, HG, D1 + 1)
        pmax = part(HG * NT, 2)
        negm = part(P)
        mrest = part(P)
        mpart = part(3, P, dt=BF16)
        trik = part(QC, dt=BF16)
        triq = part(P, dt=BF16)
        rden = part(HG * NQC)
        xn = arena[:, 4096:6144].rearrange("p (t c) -> p t c", t=NT)
        xnT = arena[:, 6144:8192]
        raw = arena[:, 12288:14336]
        parts_q, parts_k = ([arena[:, o + 1024 * i:o + 1024 * (i + 1)].bitcast(BF16) for i in range(3)]
                            for o in (14336, 17408))
        z = arena[:, 0:2048].rearrange("p (t c) -> p t c", t=NT)
        zsq = arena[:, 2048:4096].rearrange("p (t c) -> p t c", t=NT)
        y1T = arena[:, 4096:6144]

        used[0] = 0
        xcur = part(P)
        xsT = part(W + P + 1)
        part(3)
        qkn = part(2, H, DH)
        rots = part(2, H, DH)
        sq = part(2 * H * DH)
        qT = part(8, P)
        kT = part(8, W + P)
        vv = part(WPT, 8, DH)
        prob = part(8, 2, 2 * W)
        probT = part(8, P)
        att = part(8, 2, DH)
        attT = part(8, P)
        ss = part(2 * H)
        rt = part(2 * H)
        rn = part(2 * H)
        smax, ssum, rsum = part(H), part(H), part(H)
        xm = part(P)
        xmT = part(P + 2)
        xc, xcg, xsq, var, dev, rstd = (part(P) for _ in range(6))
        hg = part(2 * FF)
        gg = part(FF)
        gated = part(FF)
        hT = part(3, P)

        w_in = sb("w_in", [P, 4, C])
        b_qk = sb("b_qk", [P, 2])
        b_vo = sb("b_vo", [P, 2, C])

        all_done = sem("all_done")
        attT_read = sem("attT_read")
        attT_ready = sem("attT_ready")
        att_ready = sem("att_ready")
        back_read = sem("back_read")
        back_ready = sem("back_ready")
        carry_zero = sem("carry_zero")
        const_in = sem("const_in")
        cos_ready = sem("cos_ready")
        den_ready = sem("den_ready")
        dev_ready = sem("dev_ready")
        exp_done = sem("exp_done")
        gelu_ready = sem("gelu_ready")
        hT_read = sem("hT_read")
        hT_ready = sem("hT_ready")
        h_read = sem("h_read")
        h_ready = sem("h_ready")
        hh_ready = sem("hh_ready")
        ident_in = sem("ident_in")
        identb_ready = sem("identb_ready")
        ln_step = sem("ln_step")
        max_in = sem("max_in")
        max_out = sem("max_out")
        max_step = sem("max_step")
        mpart_ready = sem("mpart_ready")
        negmT_ready = sem("negmT_ready")
        negm_ready = sem("negm_ready")
        oT_read = sem("oT_read")
        oT_ready = sem("oT_ready")
        o_read = sem("o_read")
        ones_in = sem("ones_in")
        out_done = sem("out_done")
        pT_read = sem("pT_read")
        pT_ready = sem("pT_ready")
        parts_out = sem("parts_out")
        parts_ready = sem("parts_ready")
        pattern_ready = sem("pattern_ready")
        piece_read = sem("piece_read")
        piece_ready = sem("piece_ready")
        pv_done = sem("pv_done")
        pv_ready = sem("pv_ready")
        qkT_read = sem("qkT_read")
        qkT_ready = sem("qkT_ready")
        qk_proj = sem("qk_proj")
        qk_read = sem("qk_read")
        qk_ready = sem("qk_ready")
        qk_sq = sem("qk_sq")
        qkn_ready = sem("qkn_ready")
        rn_ready = sem("rn_ready")
        rot_ready = sem("rot_ready")
        rstd_ready = sem("rstd_ready")
        rt_ready = sem("rt_ready")
        s_exp = sem("s_exp")
        s_max = sem("s_max")
        s_ready = sem("s_ready")
        s_rsum = sem("s_rsum")
        s_sub = sem("s_sub")
        s_sum = sem("s_sum")
        score_ready = sem("score_ready")
        sin_ready = sem("sin_ready")
        sqrt_ready = sem("sqrt_ready")
        ss_ready = sem("ss_ready")
        ss_step = sem("ss_step")
        stack_clear = sem("stack_clear")
        stack_in = sem("stack_in")
        sumsq_ready = sem("sumsq_ready")
        v_proj = sem("v_proj")
        v_read = sem("v_read")
        v_ready = sem("v_ready")
        var_read = sem("var_read")
        var_ready = sem("var_ready")
        vaug_ready = sem("vaug_ready")
        vcur_ready = sem("vcur_ready")
        vec_step = sem("vec_step")
        w2_ready = sem("w2_ready")
        w_in_in = sem("w_in_in")
        w_loaded = sem("w_loaded")
        wo_ready = sem("wo_ready")
        wv_loaded = sem("wv_loaded")
        xT_ready = sem("xT_ready")
        x_done = sem("x_done")
        x_in = sem("x_in")
        x_low = sem("x_low")
        x_step = sem("x_step")
        xb_ready = sem("xb_ready")
        xc_read = sem("xc_read")
        xc_ready = sem("xc_ready")
        xcur_ready = sem("xcur_ready")
        xmT_read = sem("xmT_read")
        xmT_ready = sem("xmT_ready")
        xm_ready = sem("xm_ready")
        xm_step = sem("xm_step")
        xnT_read = sem("xnT_read")
        xnT_ready = sem("xnT_ready")
        xn_ready = sem("xn_ready")
        xnf_ready = sem("xnf_ready")
        xs_ready = sem("xs_ready")
        xsq_ready = sem("xsq_ready")
        yT_read = sem("yT_read")
        yT_ready = sem("yT_ready")
        z_read = sem("z_read")
        z_ready = sem("z_ready")

        NW = 7
        NCONST = 13
        NSTACK = 19
        block = ctx.enter_context(nc.Block())

        def weights(sp, l, w):
            one = lambda n: a[n][bass.ds(l, 1)]
            slot = bass.ds(w, 1)
            for o, i in (
                (wqk[:, slot], one("L0_ffn_Wqkv")[:, :, 0:2 * INNER].rearrange("l c n -> c l n")),
                (wo[:, slot], one("L0_ffn_Wo").rearrange("l (k p) n -> p l k n", p=P)),
                (w1[:, slot], one("L0_ffn_W1").rearrange("l c n -> c l n")),
                (w2[:, slot, 0:2], one("L0_ffn_W2")[:, 0:2 * P].rearrange("l (k p) n -> p l k n", p=P)),
                (w2[0:FF - 2 * P, slot, 2], one("L0_ffn_W2")[:, 2 * P:FF].rearrange("l p n -> p l n")),
                (b1[:, slot], one("L0_ffn_b1").partition_broadcast(P)),
                (b2[:, slot], one("L0_ffn_b2").partition_broadcast(P)),
            ):
                sp.dma_start(o, i).then_inc(w_loaded, 16)

        def weights_v(sp, l):
            sp.dma_start(wv[:, :], a["L0_ffn_Wqkv"][bass.ds(l, 1), :, 2 * INNER:3 * INNER].rearrange("l c n -> c (l n)")).then_inc(wv_loaded, 16)

        def flat(eng, it):
            it(0, True, False, False)
            it(1, True, True, False)
            it(2, True, True, True)
            with eng.Fori(3, NTILE) as n:
                it(n, True, True, True)
            it(NTILE, False, True, True)
            it(NTILE + 1, False, False, True)

        def tab(l, cs):
            return table[:, bass.ds(l, 1), :, cs, :].rearrange("p l s d -> p s l d")

        def first_query(qc, kt):
            return P * max(0, kt - QC // P * qc) if qc else 0

        @block.sync
        def _(sp):
            sp.dma_start(x[:, :, :], a["L0_attn_x"].rearrange("b (t p) c -> p (b t) c", p=P)).then_inc(x_in, 16)
            for i, n in enumerate("qkvo"):
                sp.dma_start(w_in[:, i, :], a[f"L0_attn_W{n}"]).then_inc(w_in_in, 16)
            for i, n in enumerate("qk"):
                sp.dma_start(b_qk[:, i:i + 1], a[f"L0_attn_b{n}"].rearrange("(p o) -> p o", o=1)).then_inc(w_in_in, 16)
            for i, n in enumerate("vo"):
                sp.dma_start(b_vo[:, i, :], a[f"L0_attn_b{n}"].partition_broadcast(P)).then_inc(w_in_in, 16)
            for s, p3 in ((0, parts_q), (1, parts_k)):
                for i in range(3):
                    sp.wait_ge(parts_ready, 3 * s + i + 1)
                    sp.dma_start(qk_parts[s, i], p3[i]).then_inc(parts_out, 16)
            sp.wait_ge(parts_out, 96)

            def stack(g, slot):
                for i in range(3):
                    for j in range(3):
                        r = (3 * i + j) * D1
                        for s, n, dst in ((0, i, qst), (1, j, kst)):
                            src = qk_parts[s, n].rearrange("(g h d) t -> d g h t", g=NHG, h=HG)[:, bass.ds(g, 1)]
                            sp.dma_start(dst[r:r + D1, bass.ds(slot, 1)], src).then_inc(stack_in, 16)
                sp.dma_start(qst[ROWS:ROWS + 3, bass.ds(slot, 1)],
                             a["c_zeros"].rearrange("r (s h t) -> r s h t", s=1, h=HG)).then_inc(stack_in, 16)

            def maxima(g, slot):
                sp.wait_ge(mpart_ready, g + 1)
                sp.dma_start(max_parts[bass.ds(g, 1)].rearrange("g i m q -> m (g i) q"),
                             mpart[0:HG * NT]).then_inc(max_out, 16)
                sp.wait_ge(max_out, 16 * (g + 1))
                sp.dma_start(qst[ROWS:ROWS + 3, bass.ds(slot, 1)],
                             max_parts[bass.ds(g, 1)].rearrange("g i (h t) q -> i g h (t q)", h=HG)).then_inc(max_in, 16)

            for s in range(2):
                sp.wait_ge(stack_clear, 2 * (s + 1))
                sp.dma_start(kst[ROWS:ROWS + 3, s], a["c_ones"].rearrange("r (h t) -> r h t", h=HG)).then_inc(ones_in, 16)
                stack(s, s)
                sp.wait_ge(ones_in, 16 * (s + 1))
                sp.wait_ge(stack_in, 16 * NSTACK * (s + 1))
            weights(sp, 0, 0)
            weights_v(sp, 0)
            sp.wait_ge(w_loaded, 16 * NW)
            weights(sp, 1, 1)
            maxima(0, 0)
            with sp.Fori(1, NHG - 1) as g:
                maxima(g, g % 2)
                sp.wait_ge(pv_done, NS * g)
                stack(g + 1, (g + 1) % 2)
            maxima(NHG - 1, (NHG - 1) % 2)
            with sp.Fori(1, L - 1) as l:
                sp.wait_ge(v_proj, WPT * NT * l)
                weights_v(sp, l)
                sp.wait_ge(w2_ready, NT * l)
                sp.wait_ge(x_done, NT * (l + 1))
                weights(sp, l + 1, (l + 1) % 2)
            sp.wait_ge(v_proj, WPT * NT * (L - 1))
            weights_v(sp, L - 1)
            sp.wait_ge(all_done, 1)
            sp.dma_start(out.rearrange("b (t p) c -> p (b t) c", p=P), x[:, :, :]).then_inc(out_done, 16)
            sp.wait_ge(out_done, 16)

        @block.gpsimd
        def _(gp):
            gp.dma_start(ident[:, :], a["c_ident"]).then_inc(ident_in, 16)
            for dst, n in ((rot[:, :, :], "rot"), (back[:, :], "back"), (centre[:, :], "centre"), (mean[:, :], "mean"),
                           (pattern[:, :], "pattern"), (select[:, :, :], "select"), (carry[:, :], "carry"),
                           (trik, "tri_k"), (triq, "tri_q")):
                gp.dma_start(dst, a[f"c_{n}"]).then_inc(const_in, 16)
            with nc.allow_non_contiguous_dma(reason="a column a layer"):
                gp.dma_start(ln_g[:, :], a["L0_ffn_ln_g"].rearrange("l c -> c l")).then_inc(const_in, 16)
                gp.dma_start(ln_b[:, :], a["L0_ffn_ln_b"].rearrange("l c -> c l")).then_inc(const_in, 16)
            for i, n in enumerate(("q_scale", "k_scale")):
                gp.dma_start(qks[:, i], a[f"L0_ffn_{n}"].partition_broadcast(P)).then_inc(const_in, 16)

            gp.memset(arena[64:P, 0:4096], 0.0).then_inc(stack_clear, 1)
            gp.memset(arena[64:P, 8192:12288], 0.0).then_inc(stack_clear, 1)
            gp.wait_ge(parts_out, 96)
            gp.wait_ge(v_ready, 4)
            gp.memset(arena[64:P, 4096:8192], 0.0).then_inc(stack_clear, 1)
            gp.memset(arena[64:P, 12288:16384], 0.0).then_inc(stack_clear, 1)

            def it(n, A, B, F):
                if A:
                    gp.wait_ge(qkn_ready, n + 1)
                    gp.wait_ge(rot_ready, n)
                    for o, i in ((0, DH // 2), (DH // 2, 0)):
                        gp.tensor_tensor(rots[:, :, :, o:o + DH // 2], qkn[:, :, :, i:i + DH // 2],
                                         tab(n // NT, 1)[:, :, :, o:o + DH // 2].to_broadcast([P, 2, H, DH // 2]),
                                         ALU.mult).then_inc(sin_ready, 1)

            flat(gp, it)

        @block.scalar
        def _(act):
            def norm_sqrt(i):
                act.wait_ge(sumsq_ready, i + 1)
                act.activation(stat[:, 5, :], stat[:, 4, :], ACT.Sqrt).then_inc(sqrt_ready, 1)

            norm_sqrt(0)
            for b in range(4):
                act.wait_ge(xnT_ready, b + 1)
                act.activation(xnT[:, 512 * b:512 * b + 512], bank[:, b, :], ACT.Copy).then_inc(xnT_read, 1)
            act.wait_ge(w_in_in, 128)
            for s in range(2):
                if s:
                    act.wait_ge(parts_ready, 3)
                for b in range(4):
                    act.wait_ge(qk_ready, 4 * s + b + 1)
                    act.activation(raw[:, 512 * b:512 * b + 512], bank[:, (4 - 4 * s) + b, :], ACT.Identity,
                                   bias=b_qk[:, s:s + 1]).then_inc(qk_read, 1)

            def exps(k):
                for s, (qc, kt) in enumerate(steps):
                    lo = first_query(qc, kt)
                    for h in range(HG):
                        u = HG * s + h
                        act.wait_ge(score_ready, HG * NS * k + u + 1)
                        if h == 0:
                            act.wait_ge(pv_done, NS * k + (s - 1 if s >= 2 else 0))
                        act.activation(ring[:, u % 8, lo:QC], bank[:, 4 + u % 3, lo:QC], ACT.Exp,
                                       scale=SCALE1).then_inc(exp_done, 1)

            exps(0)
            with act.Fori(1, NHG) as k:
                exps(k)
            for b in range(4):
                act.wait_ge(yT_ready, b + 1)
                act.activation(y1T[:, 512 * b:512 * b + 512], bank[:, b, :], ACT.Copy).then_inc(yT_read, 1)
            norm_sqrt(1)
            norm_sqrt(2)

            def it(n, A, B, F):
                k = n - 2
                if A:
                    act.wait_ge(qk_proj, n + 1)
                    act.wait_ge(rot_ready, n)
                    act.activation(sq, bank[:, 0:4, :].rearrange("p b n -> p (b n)"), ACT.Square).then_inc(qk_sq, 1)
                if B:
                    for i in range(2):
                        act.wait_ge(pT_ready, 2 * (n - 1) + i + 1)
                        act.wait_ge(pv_ready, n - 1)
                        act.activation(probT[:, 4 * i:4 * i + 4, :], bank[:, 4 + i, :].rearrange("p (k t) -> p k t", k=4),
                                       ACT.Copy).then_inc(pT_read, 1)
                if A:
                    act.wait_ge(ss_ready, n + 1)
                    act.wait_ge(rn_ready, n)
                    act.activation(rt[:, :], ss[:, :], ACT.Sqrt).then_inc(rt_ready, 1)
                if F:
                    act.wait_ge(var_read, k + 1)
                    act.wait_ge(rstd_ready, k)
                    act.activation(dev[:, :], var[:, :], ACT.Sqrt).then_inc(dev_ready, 1)
                if A:
                    for j in range(WPT):
                        act.wait_ge(v_proj, 4 * n + j + 1)
                        act.wait_ge(pv_ready, n)
                        act.activation(vv[:, j], bank[:, 6 + j % 2, :].rearrange("p (k d) -> p k d", k=8),
                                       ACT.Copy).then_inc(v_read, 1)
                if B:
                    for i in range(2):
                        act.wait_ge(attT_ready, 2 * (n - 1) + i + 1)
                        act.wait_ge(wo_ready, n - 1)
                        act.activation(attT[:, 4 * i:4 * i + 4, :], bank[:, 4 + i, :].rearrange("p (k t) -> p k t", k=4),
                                       ACT.Copy).then_inc(attT_read, 1)
                if F:
                    act.wait_ge(h_read, k + 1)
                    act.wait_ge(hh_ready, k)
                    act.activation(gg[:, :], hg[:, FF:2 * FF], ACT.Gelu).then_inc(gelu_ready, 1)
                if A:
                    act.wait_ge(back_ready, n + 1)
                    act.wait_ge(s_ready, n)
                    act.activation(kT[:, :, 0:W], bank[:, 7, 0:8 * W].rearrange("p (k t) -> p k t", k=8),
                                   ACT.Copy).then_inc(back_read, 1)
                    for b in range(4):
                        act.wait_ge(qkT_ready, 4 * n + b + 1)
                        dst = qT[:, 4 * b:4 * b + 4, :] if b < 2 else kT[:, 4 * b - 8:4 * b - 4, W:W + P]
                        act.activation(dst, bank[:, b, :].rearrange("p (k t) -> p k t", k=4), ACT.Copy).then_inc(qkT_read, 1)
                if F:
                    act.wait_ge(hT_ready, k + 1)
                    act.wait_ge(w2_ready, k)
                    act.activation(hT[:, 0:2, :], bank[:, 4, 0:2 * P].rearrange("p (k t) -> p k t", k=2),
                                   ACT.Copy).then_inc(hT_read, 1)
                    act.activation(hT[0:FF - 2 * P, 2, :], bank[0:FF - 2 * P, 4, 2 * P:3 * P], ACT.Copy).then_inc(hT_read, 1)
                if B:
                    act.wait_ge(xc_read, n)
                    act.wait_ge(var_ready, n - 1)
                    act.activation(xsq[:, :], xc[:, :], ACT.Square).then_inc(xsq_ready, 1)
                if A:
                    act.wait_ge(s_sub, n + 1)
                    act.activation(prob[:, :, :, :], prob[:, :, :, :], ACT.Exp).then_inc(s_exp, 1)

            flat(act, it)
            norm_sqrt(3)

        @block.tensor
        def _(pe):
            mm = pe.matmul
            pe.wait_ge(ident_in, 16)
            for t in range(NT):
                if t == 0:
                    pe.wait_ge(xn_ready, 1)
                last = pe.transpose(bank[:, t // 4, P * (t % 4):P * (t % 4) + P], xn[:, t, :], ident[:, :])
                if t % 4 == 3:
                    last.then_inc(xnT_ready, 1)
            pe.wait_ge(w_in_in, 128)
            for s in range(2):
                for b in range(4):
                    pe.wait_ge(xnT_read, b + 1)
                    mm(bank[:, 4 - 4 * s + b, :], w_in[:, s, :], xnT[:, 512 * b:512 * b + 512],
                       start=True, stop=True).then_inc(qk_ready, 1)
            for t in range(NT):
                pe.wait_ge(qk_read, t // 4 + 1)
                last = mm(bank[:, 4 + t // 4, P * (t % 4):P * (t % 4) + P], xnT[:, P * t:P * t + P], w_in[:, 2, :],
                          start=True, stop=True)
                if t % 4 == 3:
                    last.then_inc(v_ready, 1)

            def scores_for_max(k, slot, i):
                h, t, c = pieces[i]
                pe.wait_ge(piece_read, NPC * k + (i - 1 if i >= 2 else 0))
                if i == 0:
                    pe.wait_ge(mpart_ready, k)
                keys = P * (t + 1)
                lo, hi = 1024 * c, min(keys, 1024 * (c + 1))
                for j in range(lo, hi, 512):
                    n = min(512, hi - j)
                    b = 2 * (i % 2) + (j - lo) // 512
                    diagonal = j + n == keys
                    last = mm(bank[:, b, 0:n], qst[:, bass.ds(slot, 1), h, P * t:P * t + P],
                              kst[:, bass.ds(slot, 1), h, j:j + n], start=True, stop=True)
                    if diagonal:
                        last = mm(bank[:, b, n - P:n], identb[:, :], triq, start=False, stop=True, skip_group_check=True)
                last.then_inc(piece_ready, 1)

            def turn_maxima(k):
                pe.wait_ge(negm_ready, k + 1)
                pe.transpose(bank[:, 0, 0:P], negm, ident[:, :]).then_inc(negmT_ready, 1)

            def scores(k, slot, s):
                qc, kt = steps[s]
                lo = first_query(qc, kt)
                if s == 0:
                    pe.wait_ge(max_in, 16 * (k + 1))
                for h in range(HG):
                    u = HG * s + h
                    b = 4 + u % 3
                    pe.wait_ge(exp_done, HG * NS * k + (u - 2 if u >= 3 else 0))
                    r = kt - QC // P * qc
                    last = mm(bank[:, b, lo:QC], kst[:, bass.ds(slot, 1), h, P * kt:P * kt + P],
                              qst[:, bass.ds(slot, 1), h, QC * qc + lo:QC * qc + QC], start=True, stop=True)
                    if r >= 0:
                        hi = P * (r + 1)
                        last = mm(bank[:, b, lo:hi], identb[:, :], trik[:, QC - hi + lo:QC], start=False, stop=True,
                                  skip_group_check=True)
                    last.then_inc(score_ready, 1)

            def values(k, s):
                qc, kt = steps[s]
                lo = first_query(qc, kt)
                pe.wait_ge(exp_done, HG * NS * k + HG * (s + 1))
                if s == 0:
                    pe.wait_ge(vcur_ready, k + 1)
                if kt == 0:
                    pe.wait_ge(oT_read, NQC * k + qc)
                for h in range(HG):
                    last = mm(bank[32 * h:32 * h + D1 + 1, 7, lo:QC], vcur[:, kt, h, :], ring[:, (HG * s + h) % 8, lo:QC],
                              start=kt == 0, stop=True, skip_group_check=True)
                last.then_inc(pv_done, 1)

            def turn_output(k, qc):
                pe.wait_ge(o_read, NQC * k + qc + 1)
                for i in range(4):
                    last = pe.transpose(bank[:, 7, P * i:P * i + P], o_sb[:, P * i:P * i + P], ident[:, :])
                last.then_inc(oT_ready, 1)

            def group(k, slot, other, more):
                for what, *i in order:
                    if what == "score":
                        scores(k, slot, i[0])
                    elif what == "pv":
                        values(k, i[0])
                    elif what == "out":
                        turn_output(k, i[0])
                    elif more:
                        scores_for_max(k + 1, other, i[0])
                if more:
                    turn_maxima(k + 1)

            pe.wait_ge(identb_ready, 1)
            pe.wait_ge(vaug_ready, 5)
            pe.wait_ge(const_in, 16 * NCONST)
            pe.wait_ge(ones_in, 16)
            pe.wait_ge(stack_in, 16 * NSTACK)
            for i in range(NPC):
                scores_for_max(0, 0, i)
            turn_maxima(0)
            pe.wait_ge(ones_in, 32)
            pe.wait_ge(stack_in, 16 * NSTACK * 2)
            group(0, 0, 1, True)
            with pe.Fori(1, NHG - 1) as k:
                pe.wait_ge(stack_in, 16 * NSTACK * (k + 2))
                group(k, k % 2, (k + 1) % 2, True)
            group(NHG - 1, (NHG - 1) % 2, NHG % 2, False)

            pe.wait_ge(oT_read, NHG * NQC)
            for t in range(NT):
                last = pe.transpose(bank[:, t // 4, P * (t % 4):P * (t % 4) + P], kept[:, t, :], ident[:, :])
                if t % 4 == 3:
                    last.then_inc(yT_ready, 1)
            for t in range(NT):
                pe.wait_ge(yT_read, t // 4 + 1)
                last = mm(bank[:, 4 + t // 4, P * (t % 4):P * (t % 4) + P], y1T[:, P * t:P * t + P], w_in[:, 3, :],
                          start=True, stop=True)
                if t % 4 == 3:
                    last.then_inc(z_ready, 1)

            def it(n, A, B, F):
                wa, wb, wf = ((n - d) // NT % 2 for d in (0, 1, 2))
                k = n - 2
                if A:
                    pe.wait_ge(xs_ready, n + 1)
                    pe.wait_ge(qkT_read, 4 * n)
                    pe.wait_ge(w_loaded, 16 * NW * (n // NT + 1))
                    for b in range(4):
                        last = mm(bank[:, b, :], xsT[:, W:W + P],
                                  wqk[:, bass.ds(wa, 1), 512 * b:512 * b + 512], start=True, stop=True)
                    last.then_inc(qk_proj, 1)
                if B:
                    pe.wait_ge(s_exp, n)
                    for i in range(8):
                        last = pe.transpose(bank[:, 4 + i // 4, P * (i % 4):P * (i % 4) + P],
                                            prob[:, i].rearrange("p h c -> p (h c)"), ident[:, :])
                        if i % 4 == 3:
                            last.then_inc(pT_ready, 1)
                    pe.wait_ge(v_read, 4 * n)
                    pe.wait_ge(pT_read, 2 * n)
                if F:
                    pe.wait_ge(xsq_ready, k + 1)
                    pe.wait_ge(xs_ready, n + 1 if A else NTILE + 1)
                    mm(bank[:, 7, 0:P], mean[:, :], xsq[:, :], start=True, stop=True).then_inc(var_ready, 1)
                if B:
                    for i in range(8):
                        for j in range(WPT):
                            for odd in range(2):
                                r = DH * odd
                                last = mm(bank[W * j:W * j + W, 4 + odd, DH * i:DH * i + DH], probT[r:r + DH, i, W * j:W * j + W],
                                          vv[r:r + DH, j, i, :], start=True, stop=True)
                    last.then_inc(pv_ready, 1)
                if A:
                    pe.wait_ge(wv_loaded, 16 * (n // NT + 1))
                    wv2 = wv[:, :].rearrange("p (k h d) -> p k h d", h=2, d=DH)
                    for j in range(WPT):
                        if j >= 2:
                            pe.wait_ge(v_read, 4 * n + j - 1)
                        elif j == 1 and F:
                            pe.wait_ge(var_read, k + 1)
                        elif j == 0 and isinstance(n, int):
                            if n == 1:
                                pe.wait_ge(v_read, 4)
                            if n == 2:
                                pe.wait_ge(xmT_read, 1)
                        elif j == 0:
                            pe.wait_ge(x_done, NT - 2 + n)
                        for odd in range(2):
                            last = mm(bank[DH * odd:DH * odd + DH, 6 + j % 2, :], xsT[:, W * j:W * j + 2 * W], wv2[:, :, odd, :],
                                      start=True, stop=True)
                        last.then_inc(v_proj, 1)
                if F:
                    pe.wait_ge(xnf_ready, k + 1)
                    if A:
                        pe.wait_ge(v_read, 4 * n + 4)
                    else:
                        pe.wait_ge(var_read, k + 1)
                        pe.wait_ge(x_done, NT - 2 + n)
                    for i in range(2):
                        last = mm(bank[:, 6 + i, 0:FF], xcg[:, :], w1[:, bass.ds(wf, 1), FF * i:FF * i + FF],
                                  start=True, stop=True)
                    last.then_inc(h_ready, 1)
                if B:
                    pe.wait_ge(att_ready, n)
                    for i in range(8):
                        last = pe.transpose(bank[:, 4 + i // 4, P * (i % 4):P * (i % 4) + P],
                                            att[:, i].rearrange("p h d -> p (h d)"), ident[:, :])
                        if i % 4 == 3:
                            last.then_inc(attT_ready, 1)
                    if F:
                        pe.wait_ge(h_read, k + 1)
                    else:
                        pe.wait_ge(v_read, 4 * n + 4)
                    for i in range(8):
                        if i % 4 == 0:
                            pe.wait_ge(attT_read, 2 * (n - 1) + i // 4 + 1)
                        last = mm(bank[:, 6, 0:P], attT[:, i, :], wo[:, bass.ds(wb, 1), i, :], start=i == 0, stop=i == 7)
                    last.then_inc(wo_ready, 1)
                if A:
                    if F:
                        pe.wait_ge(h_read, k + 1)
                    else:
                        pe.wait_ge(v_read, 4 * n + 4)
                    if isinstance(n, int) and n == 0:
                        pe.wait_ge(carry_zero, 1)
                    mm(bank[:, 7, 0:8 * W], back[:, :], kT[:, :, P:P + W], start=True, stop=True).then_inc(back_ready, 1)
                    pe.wait_ge(rot_ready, n + 1)
                    for i in range(16):
                        src = qkn[:, i // 8, 2 * (i % 8):2 * (i % 8) + 2, :].rearrange("p h d -> p (h d)")
                        last = pe.transpose(bank[:, i // 4, P * (i % 4):P * (i % 4) + P], src, ident[:, :])
                        if i % 4 == 3:
                            last.then_inc(qkT_ready, 1)
                if B:
                    pe.wait_ge(xm_ready, n)
                    pe.transpose(bank[:, 6, 0:P], xm[:, :], ident[:, :]).then_inc(xmT_ready, 1)
                if A:
                    pe.wait_ge(xcur_ready, n + 2)
                    pe.wait_ge(back_read, n + 1)
                    pe.transpose(bank[:, 7, 0:P], xcur[:, :], ident[:, :]).then_inc(xT_ready, 1)
                if F:
                    pe.wait_ge(hh_ready, k + 1)
                    pe.wait_ge(attT_read, 2 * n if B else 2 * NTILE)
                    for i in range(3):
                        m = min(P, FF - P * i)
                        last = pe.transpose(bank[0:m, 4, P * i:P * i + P], gated[:, P * i:P * i + m], ident[:, :])
                    last.then_inc(hT_ready, 1)
                if B:
                    pe.wait_ge(xmT_read, n)
                    pe.wait_ge(attT_read, 2 * n)
                    mm(bank[:, 5, 0:P], centre[:, :], xmT[:, 0:P], start=True, stop=True).then_inc(xc_ready, 1)
                if F:
                    pe.wait_ge(hT_read, 2 * (k + 1))
                    pe.wait_ge(xmT_read, n if B else NTILE)
                    for i in range(3):
                        m = min(P, FF - P * i)
                        last = mm(bank[:, 6, 0:P], hT[0:m, i, :], w2[0:m, bass.ds(wf, 1), i, :], start=i == 0, stop=i == 2)
                    last.then_inc(w2_ready, 1)
                if A:
                    if F:
                        pe.wait_ge(hT_read, 2 * (k + 1))
                    if B:
                        pe.wait_ge(xc_read, n)
                    pe.wait_ge(back_read, n + 1)
                    pe.wait_ge(qkT_read, 4 * n + 4)
                    if isinstance(n, int) and n == 0:
                        pe.wait_ge(pattern_ready, 1)
                    for odd in range(2):
                        mm(bank[:, 4 + odd, :], select[:, bass.ds(n % NT, 1), :], pattern8[:, :, :], start=True, stop=True)
                    for i in range(8):
                        for j in range(WPT):
                            for odd in range(2):
                                r = DH * odd
                                last = mm(bank[W * j:W * j + W, 4 + odd, 2 * W * i:2 * W * i + 2 * W],
                                          qT[r:r + DH, i, W * j:W * j + W], kT[r:r + DH, i, W * j:W * j + 2 * W],
                                          start=False, stop=True, skip_group_check=True)
                    last.then_inc(s_ready, 1)

            pe.wait_ge(xcur_ready, 1)
            pe.wait_ge(z_read, 4)
            pe.transpose(bank[:, 7, 0:P], xcur[:, :], ident[:, :]).then_inc(xT_ready, 1)
            flat(pe, it)

        @block.vector
        def _(ve):
            count = [0]

            def step(ins):
                count[0] += 1
                ins.then_inc(vec_step, 1)
                ve.wait_ge(vec_step, count[0])

            def over(s, n):
                return stat[:, s, :].unsqueeze(2).to_broadcast([P, NT, n])

            def norm(i, src, dst, work):
                step(ve.tensor_reduce(stat[:, 0, :], src, AX.X, ALU.add))
                step(ve.tensor_scalar(stat[:, 1, :], stat[:, 0, :], -1.0 / C, None, ALU.mult))
                step(ve.tensor_tensor(dst, src, over(1, C), ALU.add))
                step(ve.tensor_tensor(work, dst, dst, ALU.mult))
                step(ve.tensor_reduce(stat[:, 3, :], work, AX.X, ALU.add))
                ve.tensor_scalar(stat[:, 4, :], stat[:, 3, :], 1.0 / C, EPS, ALU.mult, ALU.add).then_inc(sumsq_ready, 1)
                ve.wait_ge(sqrt_ready, i + 1)
                step(ve.reciprocal(stat[:, 4, :], stat[:, 5, :]))

            ve.wait_ge(x_in, 16)
            norm(0, x[:, :, :], xn, raw.rearrange("p (t c) -> p t c", t=NT))
            ve.tensor_tensor(xn, xn, over(4, C), ALU.mult).then_inc(xn_ready, 1)
            ve.wait_ge(ident_in, 16)
            ve.tensor_copy(identb[:, :], ident[:, :]).then_inc(identb_ready, 1)
            step(ve.memset(vaug[:, :, :, D1:D1 + 1], 1.0))
            step(ve.memset(pmax, NEG))
            step(ve.memset(negm, 0.0))
            ve.wait_ge(const_in, 16 * NCONST)
            half = DH // 2
            for s in range(2):
                for cs, o, i, m in ((0, 0, 0, DH), (1, 0, half, half), (1, half, 0, half)):
                    step(ve.tensor_tensor(table[:, :, s, cs, o:o + m], qks[:, s, :, i:i + m],
                                          rot[:, 2 * s + cs:2 * s + cs + 1, o:o + m].to_broadcast([P, L, m]), ALU.mult))
            ve.tensor_copy(pattern8[:, :, :], pattern[:, :].unsqueeze(1).to_broadcast([P, 8, 2 * W])).then_inc(pattern_ready, 1)
            for s, p3 in ((0, parts_q), (1, parts_k)):
                ve.wait_ge(qk_read, 4 * (s + 1))
                for i in range(3):
                    ve.tensor_copy(p3[i], raw).then_inc(parts_ready, 1)
                    if i < 2:
                        ve.wait_ge(parts_ready, 3 * s + i + 1)
                        step(ve.tensor_tensor(raw, raw, p3[i], ALU.subtract))
            ve.wait_ge(w_in_in, 128)
            for b in range(4):
                ve.wait_ge(v_ready, b + 1)
                bias = b_vo[:, 0:1, :].rearrange("p o (h d) -> p o h d", h=H1).to_broadcast([P, 4, H1, D1])
                ve.tensor_tensor(vaug[:, 4 * b:4 * b + 4, :, 0:D1],
                                 bank[:, 4 + b, :].rearrange("p (t h d) -> p t h d", t=4, h=H1), bias, ALU.add).then_inc(vaug_ready, 1)
            ve.wait_ge(vaug_ready, 4)
            ve.memset(bank[:, 7, :], 0.0).then_inc(vaug_ready, 1)
            ve.wait_ge(vaug_ready, 5)

            def max_piece(k, i):
                h, t, c = pieces[i]
                n = min(P * (t + 1) - 1024 * c, 1024)
                ve.wait_ge(piece_ready, NPC * k + i + 1)
                src = bank[:, 2 * (i % 2):2 * (i % 2) + 2, :].rearrange("p b n -> p (b n)")[:, 0:n]
                ve.tensor_reduce(pmax[:, h * NT + t, c:c + 1], src, AX.X, ALU.max).then_inc(piece_read, 1)

            def split_maxima(k):
                ve.wait_ge(piece_read, NPC * (k + 1))
                m = negm[:, 0:HG * NT]
                ve.tensor_reduce(m, pmax, AX.X, ALU.max).then_inc(max_step, 1)
                ve.wait_ge(max_step, 5 * k + 1)
                ve.tensor_scalar(m, m, -1.0, None, ALU.mult).then_inc(negm_ready, 1)
                ve.wait_ge(negmT_ready, k + 1)
                ve.wait_ge(max_out, 16 * k)
                ve.tensor_copy(mpart[:, 0, :], bank[:, 0, 0:P]).then_inc(max_step, 1)
                ve.wait_ge(max_step, 5 * k + 2)
                ve.tensor_tensor(mrest, bank[:, 0, 0:P], mpart[:, 0, :], ALU.subtract).then_inc(max_step, 1)
                ve.wait_ge(max_step, 5 * k + 3)
                ve.tensor_copy(mpart[:, 1, :], mrest).then_inc(max_step, 1)
                ve.wait_ge(max_step, 5 * k + 4)
                ve.tensor_tensor(mrest, mrest, mpart[:, 1, :], ALU.subtract).then_inc(max_step, 1)
                ve.wait_ge(max_step, 5 * k + 5)
                ve.tensor_copy(mpart[:, 2, :], mrest).then_inc(mpart_ready, 1)

            y = kept[:, :, :].rearrange("p t (g h d) -> p t g h d", g=NHG, h=HG)

            def group(k, more):
                ve.wait_ge(pv_done, NS * k)
                ve.tensor_copy(vcur, vaug[:, :, bass.ds(HG * k, HG), :]).then_inc(vcur_ready, 1)
                for what, *i in order:
                    if what == "pv":
                        qc, kt = steps[i[0]]
                        if kt == QC // P * (qc + 1) - 1:
                            ve.wait_ge(pv_done, NS * k + i[0] + 1)
                            ve.wait_ge(oT_ready, NQC * k + qc)
                            ve.tensor_copy(o_sb, bank[:, 7, :]).then_inc(o_read, 1)
                    elif what == "out":
                        qc = i[0]
                        o = bank[:, 7, :].rearrange("p (t h d) -> p t h d", t=4, h=HG)
                        r = rden.rearrange("p (t h o) -> p t h o", t=4, h=HG)
                        ve.wait_ge(oT_ready, NQC * k + qc + 1)
                        ve.wait_ge(oT_read, NQC * k + qc)
                        ve.reciprocal(r, o[:, :, :, D1:D1 + 1]).then_inc(den_ready, 1)
                        ve.wait_ge(den_ready, NQC * k + qc + 1)
                        dst = y[:, 4 * qc:4 * qc + 4, bass.ds(k, 1), :, :].rearrange("p t g h d -> p t (g h) d")
                        ve.tensor_tensor(dst, o[:, :, :, 0:D1], r.to_broadcast([P, 4, HG, D1]), ALU.mult).then_inc(oT_read, 1)
                    elif what == "max" and more:
                        max_piece(k + 1, i[0])
                if more:
                    split_maxima(k + 1)

            for i in range(NPC):
                max_piece(0, i)
            split_maxima(0)
            group(0, True)
            with ve.Fori(1, NHG - 1) as k:
                group(k, True)
            group(NHG - 1, False)

            for b in range(4):
                ve.wait_ge(z_ready, b + 1)
                ve.tensor_tensor(z[:, 4 * b:4 * b + 4, :], bank[:, 4 + b, :].rearrange("p (t c) -> p t c", t=4),
                                 b_vo[:, 1:2, :].to_broadcast([P, 4, C]), ALU.add).then_inc(z_read, 1)
            ve.wait_ge(z_read, 4)
            norm(1, z, z, zsq)
            step(ve.tensor_tensor(z, z, over(4, C), ALU.mult))
            step(ve.tensor_tensor(kept[:, :, :], x[:, :, :], z, ALU.add))
            norm(2, kept[:, :, :], x[:, :, :], zsq)
            for t in range(NT):
                ve.tensor_scalar(x[:, t, :], x[:, t, :], stat[:, 4, t:t + 1], None, ALU.mult).then_inc(x_done, 1)

            ve.wait_ge(x_done, NT)
            step(ve.memset(kT, 0.0))
            step(ve.memset(xsT, 0.0))
            step(ve.memset(xmT, 0.0))
            ve.memset(gated[:, :], 0.0).then_inc(carry_zero, 1)
            ve.wait_ge(carry_zero, 1)

            def x_copy(n):
                ve.wait_ge(x_done, n + 1)
                ve.wait_ge(xT_ready, n)
                ve.tensor_copy(xcur[:, :], x[:, bass.ds(n % NT, 1), :].rearrange("p o c -> p (o c)")).then_inc(xcur_ready, 1)

            def x_shift(n):
                ve.tensor_scalar(xsT[:, 0:W + 1], xsT[:, P:P + W + 1], carry[:, bass.ds(n % NT, 1)], None,
                                 ALU.mult).then_inc(x_step, 1)
                ve.wait_ge(x_step, n + 1)
                ve.wait_ge(xT_ready, n + 1)
                ve.tensor_copy(xsT[0:64, W:W + P], bank[0:64, 7, 0:P]).then_inc(x_low, 1)
                ve.wait_ge(x_low, n + 1)
                ve.tensor_copy(xsT[64:P, W + 1:W + P + 1], bank[64:P, 7, 0:P]).then_inc(xs_ready, 1)

            def it(n, A, B, F):
                wb, wf = ((n - d) // NT % 2 for d in (1, 2))
                k = n - 2
                tb, tf = (bass.ds((n - d) % NT, 1) for d in (1, 2))
                flatten = lambda v: v.rearrange("p o c -> p (o c)")
                p4 = prob.rearrange("p k h c -> p h k c")
                by_head = lambda v: v.rearrange("p (h k) -> p h k", h=2)
                if B:
                    ve.wait_ge(s_exp, n)
                    ve.tensor_reduce(by_head(ssum), p4, AX.X, ALU.add).then_inc(s_sum, 1)
                    ve.wait_ge(s_sum, n)
                    ve.wait_ge(att_ready, n - 1)
                    ve.reciprocal(rsum[:, :], ssum[:, :]).then_inc(s_rsum, 1)
                if A:
                    ve.wait_ge(qk_sq, n + 1)
                    ve.wait_ge(rt_ready, n)
                    ve.tensor_reduce(ss[:, :], sq.rearrange("p (h d) -> p h d", d=DH), AX.X, ALU.add).then_inc(ss_step, 1)
                    ve.wait_ge(ss_step, n + 1)
                    ve.tensor_scalar(ss[:, :], ss[:, :], 1e-24, None, ALU.max).then_inc(ss_ready, 1)
                if F:
                    ve.wait_ge(var_ready, k + 1)
                    ve.wait_ge(dev_ready, k)
                    ve.tensor_scalar(var[:, :], bank[:, 7, 0:P], EPS, None, ALU.add).then_inc(var_read, 1)
                if A:
                    ve.wait_ge(rt_ready, n + 1)
                    ve.wait_ge(qkn_ready, n)
                    ve.reciprocal(rn[:, :], rt[:, :]).then_inc(rn_ready, 1)
                    ve.wait_ge(rn_ready, n + 1)
                    ve.wait_ge(qkT_ready, 4 * n)
                    ve.tensor_tensor(qkn.rearrange("p s h d -> p (s h) d"), bank[:, 0:4, :].rearrange("p b (h d) -> p (b h) d", d=DH),
                                     rn[:, :].unsqueeze(2).to_broadcast([P, 2 * H, DH]), ALU.mult).then_inc(qkn_ready, 1)
                if F:
                    ve.wait_ge(dev_ready, k + 1)
                    ve.wait_ge(xnf_ready, k)
                    ve.reciprocal(rstd[:, :], dev[:, :]).then_inc(rstd_ready, 1)
                    ve.wait_ge(rstd_ready, k + 1)
                    ve.wait_ge(h_ready, k)
                    ln = bass.ds(k // NT, 1)
                    ve.scalar_tensor_tensor(out=xcg[:, :], in0=xc[:, :], scalar=ln_g[:, ln], in1=rstd[:, :], op0=ALU.mult,
                                            op1=ALU.mult).then_inc(ln_step, 1)
                    ve.wait_ge(ln_step, k + 1)
                    ve.tensor_scalar(xcg[:, :], xcg[:, :], ln_b[:, ln], None, ALU.add).then_inc(xnf_ready, 1)
                if B:
                    ve.wait_ge(pv_ready, n)
                    ve.wait_ge(s_rsum, n)
                    ve.wait_ge(attT_ready, 2 * (n - 1))
                    ve.tensor_tensor(att.rearrange("p k h d -> p h k d"), bank[:, 4:6, :].rearrange("p b (k d) -> p b k d", d=DH),
                                     by_head(rsum).unsqueeze(3).to_broadcast([P, 2, 8, DH]), ALU.mult).then_inc(att_ready, 1)
                if A:
                    ve.wait_ge(qkn_ready, n + 1)
                    ve.tensor_tensor(sq.rearrange("p (s h d) -> p s h d", s=2, h=H), qkn,
                                     tab(n // NT, 0).to_broadcast([P, 2, H, DH]), ALU.mult).then_inc(cos_ready, 1)
                if F:
                    ve.wait_ge(h_ready, k + 1)
                    ve.wait_ge(hh_ready, k)
                    ve.tensor_tensor(hg.rearrange("p (i f) -> p i f", i=2), bank[:, 6:8, 0:FF],
                                     b1[:, bass.ds(wf, 1), :].rearrange("p o (i f) -> p (o i) f", i=2), ALU.add).then_inc(h_read, 1)
                if A:
                    ve.wait_ge(cos_ready, n + 1)
                    ve.wait_ge(sin_ready, 2 * (n + 1))
                    ve.tensor_tensor(qkn.rearrange("p s h d -> p (s h d)"), sq, rots.rearrange("p s h d -> p (s h d)"),
                                     ALU.add).then_inc(rot_ready, 1)
                if B:
                    ve.wait_ge(wo_ready, n)
                    ve.wait_ge(xmT_ready, n - 1)
                    ve.tensor_tensor(xm[:, :], bank[:, 6, 0:P], flatten(x[:, tb, :]), ALU.add).then_inc(xm_ready, 1)
                    ve.wait_ge(xm_ready, n)
                    ve.tensor_tensor(flatten(x[:, tb, :]), xm[:, :], flatten(b2[:, bass.ds(wb, 1), :]), ALU.add).then_inc(xb_ready, 1)
                if F:
                    ve.wait_ge(gelu_ready, k + 1)
                    ve.wait_ge(hT_ready, k)
                    ve.tensor_tensor(gated[:, :], hg[:, 0:FF], gg[:, :], ALU.mult).then_inc(hh_ready, 1)
                if A:
                    x_copy(n + 1)
                if B:
                    ve.wait_ge(xc_ready, n - 1)
                    ve.tensor_scalar(xmT[64:P, 0:1], xmT[64:P, P:P + 1], carry[64:P, tb], None, ALU.mult).then_inc(xm_step, 1)
                    ve.wait_ge(xmT_ready, n)
                    ve.tensor_copy(xmT[0:64, 0:P], bank[0:64, 6, 0:P]).then_inc(xm_step, 1)
                    ve.wait_ge(xm_step, 2 * n)
                    ve.tensor_copy(xmT[64:P, 1:P + 1], bank[64:P, 6, 0:P]).then_inc(xmT_read, 1)
                if A:
                    ve.wait_ge(v_proj, 4 * n + 4)
                    x_shift(n + 1)
                if B:
                    ve.wait_ge(xc_ready, n)
                    ve.wait_ge(xnf_ready, n - 1)
                    ve.wait_ge(xsq_ready, n - 1)
                    ve.tensor_copy(xc[:, :], bank[:, 5, 0:P]).then_inc(xc_read, 1)
                if F:
                    ve.wait_ge(w2_ready, k + 1)
                    ve.wait_ge(xb_ready, k + 1)
                    ve.tensor_tensor(flatten(x[:, tf, :]), bank[:, 6, 0:P], flatten(x[:, tf, :]), ALU.add).then_inc(x_done, 1)
                if A:
                    ve.wait_ge(s_ready, n + 1)
                    s4 = bank[:, 4:6, :].rearrange("p b (k c) -> p b k c", c=2 * W)
                    if B:
                        ve.wait_ge(s_sub, n)
                    ve.tensor_reduce(by_head(smax), s4, AX.X, ALU.max).then_inc(s_max, 1)
                    ve.wait_ge(s_max, n + 1)
                    ve.wait_ge(pT_ready, 2 * n)
                    ve.wait_ge(s_sum, n)
                    ve.tensor_tensor(p4, s4, by_head(smax).unsqueeze(3).to_broadcast([P, 2, 8, 2 * W]), ALU.subtract).then_inc(s_sub, 1)

            x_copy(0)
            x_shift(0)
            flat(ve, it)

            ve.wait_ge(x_done, NT + NTILE)
            ve.wait_ge(xs_ready, NTILE + 1)
            norm(3, x[:, :, :], z, zsq)
            step(ve.tensor_tensor(z, z, over(4, C), ALU.mult))
            ve.tensor_tensor(x[:, :, :], kept[:, :, :], z, ALU.add).then_inc(all_done, 1)


_INS = ["L0_attn_x"] + [f"L0_attn_{k}{n}" for n in "qkvo" for k in "Wb"] + [
    f"L0_ffn_{n}" for n in ("Wqkv", "q_scale", "k_scale", "Wo", "ln_g", "ln_b", "W1", "b1", "W2", "b2")]


def kernel(**inputs):
    import concourse.bacc as bacc
    from concourse.bass_utils import run_bass_kernel_spmd

    nc = bacc.Bacc("TRN2", target_bir_lowering=False, num_devices=1)
    arrays, aps = {}, {}
    data = {n: np.ascontiguousarray(inputs[n]) for n in _INS} | constants()
    for name, v in data.items():
        arrays[f"in_{name}"] = v
        aps[name] = nc.dram_tensor(f"in_{name}", v.shape, mybir.dt.from_np(v.dtype), kind="ExternalInput").ap()
        if v.dtype == np.uint16:
            aps[name] = aps[name].bitcast(BF16)
    out = nc.dram_tensor("out_0", (1, T, C), F32, kind="ExternalOutput").ap()
    build(nc, aps, out)
    r = run_bass_kernel_spmd(nc, [arrays], core_ids=[0])
    return r.results[0]["out_0"]
```

```python
from contextlib import ExitStack

import numpy as np
import concourse.bass as bass
from concourse import mybir

F32 = mybir.dt.float32
BF16 = mybir.dt.bfloat16
ALU = mybir.AluOpType
ACT = mybir.ActivationFunctionType
AX = mybir.AxisListType

P = 128
T, C = 2048, 128
NT = T // P
EPS = 1e-5
H1, D1 = 16, 8
HG, NHG = 4, 4
NPAIR = 9
ROWS = NPAIR * D1
QC = 512
NQC = T // QC
SCALE1 = 1.0 / float(np.sqrt(np.float32(D1)))
L, H, DH, W = 6, 16, 64, 32
INNER = H * DH
FF = int(C * 4 * 2 / 3)
WPT = P // W
NTILE = L * NT
QK_SCALE = 8.0
NEG = -3.0e38


def constants():
    half = np.arange(0, DH, 2, dtype=np.float64)
    freq = 1.0 / 10000.0 ** (half / DH)
    base = (half + 0.4 * DH) / (1.4 * DH)
    p = np.arange(P)[:, None]
    ang = np.concatenate([p * freq, p * freq], -1)
    grow = base ** (p / (W // 2))
    grow = np.concatenate([grow, grow], -1)
    sign = np.where(np.arange(DH) < DH // 2, -1.0, 1.0)
    rot = np.stack([np.cos(ang) * grow * QK_SCALE, sign * np.sin(ang) * grow * QK_SCALE,
                    np.cos(ang) / grow, sign * np.sin(ang) / grow], 1)
    c, s, g = np.cos(P * freq), np.sin(P * freq), base ** (P / (W // 2))
    back = np.zeros((P, P))
    n = DH // 2
    for h in (0, DH):
        for f in range(n):
            back[h + f, h + f] = c[f] * g[f]
            back[h + n + f, h + f] = s[f] * g[f]
            back[h + n + f, h + n + f] = c[f] * g[f]
            back[h + f, h + n + f] = -s[f] * g[f]
    centre = np.eye(P) - 1.0 / C
    a = np.arange(W)
    pattern = np.zeros((P, 2 * W))
    pattern[:W, :W] = np.where(a[None, :] < a[:, None], NEG, 0)
    pattern[W:2 * W, :W] = NEG
    pattern[:W, W:] = pattern[W:2 * W, W:] = np.where(a[None, :] > a[:, None], NEG, 0)
    select = np.zeros((P, NT, P))
    for m in range(P):
        select[m % W, :, m] = 1
    for m in range(W):
        select[m, 0, m], select[W + m, 0, m] = 0, 1
    carry = np.ones((P, NT))
    carry[:, 0] = 0
    r = np.arange(P)
    tri_q = np.where(r[None, :] > r[:, None], NEG, 0)
    tri_k = np.zeros((P, QC))
    tri_k[:, :QC - P] = NEG
    tri_k[:, QC - P:] = np.where(r[:, None] > r[None, :], NEG, 0)
    f = lambda x: np.ascontiguousarray(x, dtype=np.float32)
    b = lambda x: np.ascontiguousarray((f(x).view(np.uint32) >> 16).astype(np.uint16))
    return {
        "c_rot": f(rot), "c_back": f(back), "c_centre": f(centre), "c_pattern": b(pattern),
        "c_select": b(select), "c_carry": f(carry), "c_tri_q": b(tri_q), "c_tri_k": b(tri_k),
        "c_ident": f(np.eye(P)), "c_mean": f(np.full((P, P), 1.0 / C)),
        "c_zeros": b(np.zeros((3, HG * T))), "c_ones": b(np.ones((3, HG * T))),
    }


def schedule():
    steps = [(qc, kt) for qc in range(NQC) for kt in range(QC // P * (qc + 1))]
    pieces = [(h, t, c) for h in range(HG) for t in range(NT) for c in range(1 + (t >= NT // 2))]
    order, done = [], 0
    for s, (qc, kt) in enumerate(steps):
        order.append(("score", s))
        if s >= 1:
            order.append(("pv", s - 1))
        if s >= 2 and steps[s - 2][0] != steps[s - 1][0]:
            order.append(("out", steps[s - 2][0]))
            order[-1], order[-2] = order[-2], order[-1]
        want = len(pieces) * (s + 1) // len(steps)
        while done < want:
            order.append(("max", done))
            done += 1
    order += [("pv", len(steps) - 1), ("out", NQC - 1)]
    return steps, pieces, order


def build(nc, a, out):
    steps, pieces, order = schedule()
    NS = len(steps)
    NPC = len(pieces)
    nc.disable_value_cache = True
    with ExitStack() as ctx:
        def sb(name, shape, dt=F32):
            return ctx.enter_context(nc.sbuf_tensor(name, shape, dt))

        def sem(name):
            return ctx.enter_context(nc.semaphore(name))

        bank = ctx.enter_context(nc.psum_tensor("bank", [P, 8, 512], F32))

        qk_parts = nc.dram_tensor("qk_parts", (2, 3, P, T), BF16, kind="Internal").ap()
        max_parts = nc.dram_tensor("max_parts", (NHG, 3, HG * NT, P), BF16, kind="Internal").ap()

        x = sb("x", [P, NT, C])
        kept = sb("kept", [P, NT, C])
        ident = sb("ident", [P, P])
        identb = sb("identb", [P, P], BF16)
        stat = sb("stat", [P, 6, NT])
        wqk = sb("wqk", [P, 2, 2 * INNER])
        wv = sb("wv", [P, INNER])
        wo = sb("wo", [P, 2, 8, C])
        w1 = sb("w1", [P, 2, 2 * FF])
        w2 = sb("w2", [P, 2, 3, C])
        b1 = sb("b1", [P, 2, 2 * FF])
        b2 = sb("b2", [P, 2, C])
        ln_g = sb("ln_g", [P, L])
        ln_b = sb("ln_b", [P, L])
        rot = sb("rot", [P, 4, DH])
        qks = sb("qks", [P, 2, L, DH])
        table = sb("table", [P, L, 2, 2, DH])
        back = sb("back", [P, P])
        centre = sb("centre", [P, P])
        mean = sb("mean", [P, P])
        pattern = sb("pattern", [P, 2 * W], BF16)
        pattern8 = sb("pattern8", [P, 8, 2 * W], BF16)
        select = sb("select", [P, NT, P], BF16)
        carry = sb("carry", [P, NT])

        arena = sb("arena", [P, 26880])
        used = [0]

        def part(*shape, dt=F32):
            size = int(np.prod(shape)) // (2 if dt == BF16 else 1)
            v = arena[:, used[0]:used[0] + size]
            used[0] += size
            assert used[0] <= 26880, used
            if dt != F32:
                v = v.bitcast(dt)
            if len(shape) == 1:
                return v
            names = "abcdef"[:len(shape)]
            return v.rearrange(f"p ({' '.join(names)}) -> p {' '.join(names)}",
                               **{n: d for n, d in zip(names[1:], shape[1:])})

        qst = part(2, HG, T, dt=BF16)
        kst = part(2, HG, T, dt=BF16)
        ring = part(8, QC)
        _ = part(QC, 4)
        used[0] -= 4 * QC
        o_sb = part(QC)
        vaug = part(NT, H1, D1 + 1)
        vcur = part(NT, HG, D1 + 1)
        pmax = part(HG * NT, 2)
        negm = part(P)
        mrest = part(P)
        mpart = part(3, P, dt=BF16)
        trik = part(QC, dt=BF16)
        triq = part(P, dt=BF16)
        rden = part(HG * NQC)
        xn = arena[:, 4096:6144].rearrange("p (t c) -> p t c", t=NT)
        xnT = arena[:, 6144:8192]
        raw = arena[:, 12288:14336]
        parts_q, parts_k = ([arena[:, o + 1024 * i:o + 1024 * (i + 1)].bitcast(BF16) for i in range(3)]
                            for o in (14336, 17408))
        z = arena[:, 0:2048].rearrange("p (t c) -> p t c", t=NT)
        zsq = arena[:, 2048:4096].rearrange("p (t c) -> p t c", t=NT)
        y1T = arena[:, 4096:6144]

        used[0] = 0
        xcur = part(P)
        xsT = part(W + P + 1)
        part(3)
        qkn = part(2, H, DH)
        rots = part(2, H, DH)
        sq = part(2 * H * DH)
        qT = part(8, P)
        kT = part(8, W + P)
        vv = part(WPT, 8, DH)
        prob = part(8, 2, 2 * W)
        probT = part(8, P)
        att = part(8, 2, DH)
        attT = part(8, P)
        ss = part(2 * H)
        rt = part(2 * H)
        rn = part(2 * H)
        fetch = part(1)
        smax, ssum, rsum = part(H), part(H), part(H)
        xm = part(P)
        xmT = part(P + 2)
        xc, xcg, xsq, var, dev, rstd = (part(P) for _ in range(6))
        hg = part(2 * FF)
        gg = part(FF)
        gated = part(FF)
        hT = part(3, P)

        w_in = sb("w_in", [P, 4, C])
        b_qk = sb("b_qk", [P, 2])
        b_vo = sb("b_vo", [P, 2, C])

        all_done = sem("all_done")
        attT_read = sem("attT_read")
        attT_ready = sem("attT_ready")
        att_ready = sem("att_ready")
        back_read = sem("back_read")
        back_ready = sem("back_ready")
        carry_zero = sem("carry_zero")
        const_in = sem("const_in")
        cos_ready = sem("cos_ready")
        den_ready = sem("den_ready")
        dev_ready = sem("dev_ready")
        exp_done = sem("exp_done")
        gelu_ready = sem("gelu_ready")
        hT_read = sem("hT_read")
        hT_ready = sem("hT_ready")
        h_read = sem("h_read")
        h_ready = sem("h_ready")
        hh_ready = sem("hh_ready")
        ident_in = sem("ident_in")
        identb_ready = sem("identb_ready")
        ln_step = sem("ln_step")
        max_in = sem("max_in")
        max_out = sem("max_out")
        max_step = sem("max_step")
        mpart_ready = sem("mpart_ready")
        negmT_ready = sem("negmT_ready")
        negm_ready = sem("negm_ready")
        oT_read = sem("oT_read")
        oT_ready = sem("oT_ready")
        o_read = sem("o_read")
        ones_in = sem("ones_in")
        out_done = sem("out_done")
        pT_read = sem("pT_read")
        pT_ready = sem("pT_ready")
        parts_out = sem("parts_out")
        parts_ready = sem("parts_ready")
        pattern_ready = sem("pattern_ready")
        piece_read = sem("piece_read")
        piece_ready = sem("piece_ready")
        pv_done = sem("pv_done")
        pv_ready = sem("pv_ready")
        qkT_read = sem("qkT_read")
        qkT_ready = sem("qkT_ready")
        qk_proj = sem("qk_proj")
        qk_read = sem("qk_read")
        qk_ready = sem("qk_ready")
        qk_sq = sem("qk_sq")
        qkn_ready = sem("qkn_ready")
        rn_ready = sem("rn_ready")
        rot_ready = sem("rot_ready")
        rstd_ready = sem("rstd_ready")
        rt_ready = sem("rt_ready")
        s_exp = sem("s_exp")
        s_max = sem("s_max")
        s_ready = sem("s_ready")
        s_rsum = sem("s_rsum")
        s_sub = sem("s_sub")
        s_sum = sem("s_sum")
        score_ready = sem("score_ready")
        sin_ready = sem("sin_ready")
        sqrt_ready = sem("sqrt_ready")
        ss_ready = sem("ss_ready")
        ss_step = sem("ss_step")
        stack_clear = sem("stack_clear")
        stack_in = sem("stack_in")
        sumsq_ready = sem("sumsq_ready")
        v_proj = sem("v_proj")
        v_read = sem("v_read")
        v_ready = sem("v_ready")
        var_read = sem("var_read")
        var_ready = sem("var_ready")
        vaug_ready = sem("vaug_ready")
        vcur_ready = sem("vcur_ready")
        vec_step = sem("vec_step")
        w2_ready = sem("w2_ready")
        w_in_in = sem("w_in_in")
        w_loaded = sem("w_loaded")
        wo_ready = sem("wo_ready")
        wv_loaded = sem("wv_loaded")
        xT_ready = sem("xT_ready")
        x_done = sem("x_done")
        x_in = sem("x_in")
        x_low = sem("x_low")
        x_step = sem("x_step")
        xb_ready = sem("xb_ready")
        xc_read = sem("xc_read")
        xc_ready = sem("xc_ready")
        xcur_ready = sem("xcur_ready")
        xmT_read = sem("xmT_read")
        xmT_ready = sem("xmT_ready")
        xm_ready = sem("xm_ready")
        xm_step = sem("xm_step")
        xnT_read = sem("xnT_read")
        xnT_ready = sem("xnT_ready")
        xn_ready = sem("xn_ready")
        xnf_ready = sem("xnf_ready")
        xs_ready = sem("xs_ready")
        xsq_ready = sem("xsq_ready")
        yT_read = sem("yT_read")
        yT_ready = sem("yT_ready")
        z_read = sem("z_read")
        z_ready = sem("z_ready")

        NW = 7
        NCONST = 13
        NSTACK = 19
        block = ctx.enter_context(nc.Block())

        def weights(sp, l, w):
            one = lambda n: a[n][bass.ds(l, 1)]
            slot = bass.ds(w, 1)
            for o, i in (
                (wqk[:, slot], one("L0_ffn_Wqkv")[:, :, 0:2 * INNER].rearrange("l c n -> c l n")),
                (wo[:, slot], one("L0_ffn_Wo").rearrange("l (k p) n -> p l k n", p=P)),
                (w1[:, slot], one("L0_ffn_W1").rearrange("l c n -> c l n")),
                (w2[:, slot, 0:2], one("L0_ffn_W2")[:, 0:2 * P].rearrange("l (k p) n -> p l k n", p=P)),
                (w2[0:FF - 2 * P, slot, 2], one("L0_ffn_W2")[:, 2 * P:FF].rearrange("l p n -> p l n")),
                (b1[:, slot], one("L0_ffn_b1").partition_broadcast(P)),
                (b2[:, slot], one("L0_ffn_b2").partition_broadcast(P)),
            ):
                sp.dma_start(o, i).then_inc(w_loaded, 16)

        def weights_v(sp, l):
            sp.dma_start(wv[:, :], a["L0_ffn_Wqkv"][bass.ds(l, 1), :, 2 * INNER:3 * INNER].rearrange("l c n -> c (l n)")).then_inc(wv_loaded, 16)

        def flat(eng, it):
            it(0, True, False, False, False)
            it(1, True, True, False, False)
            it(2, True, True, True, False)
            it(3, True, True, True, True)
            with eng.Fori(4, NTILE) as n:
                it(n, True, True, True, True)
            it(NTILE, False, True, True, True)
            it(NTILE + 1, False, False, True, True)
            it(NTILE + 2, False, False, False, True)

        def tab(l, s, cs):
            return table[:, bass.ds(l, 1), s, cs, :]

        def first_query(qc, kt):
            return P * max(0, kt - QC // P * qc) if qc else 0

        @block.sync
        def _(sp):
            sp.dma_start(x[:, :, :], a["L0_attn_x"].rearrange("b (t p) c -> p (b t) c", p=P)).then_inc(x_in, 16)
            for i, n in enumerate("qkvo"):
                sp.dma_start(w_in[:, i, :], a[f"L0_attn_W{n}"]).then_inc(w_in_in, 16)
            for i, n in enumerate("qk"):
                sp.dma_start(b_qk[:, i:i + 1], a[f"L0_attn_b{n}"].rearrange("(p o) -> p o", o=1)).then_inc(w_in_in, 16)
            for i, n in enumerate("vo"):
                sp.dma_start(b_vo[:, i, :], a[f"L0_attn_b{n}"].partition_broadcast(P)).then_inc(w_in_in, 16)
            for s, p3 in ((0, parts_q), (1, parts_k)):
                for i in range(3):
                    sp.wait_ge(parts_ready, 3 * s + i + 1)
                    sp.dma_start(qk_parts[s, i], p3[i]).then_inc(parts_out, 16)
            sp.wait_ge(parts_out, 96)

            def stack(g, slot):
                for i in range(3):
                    for j in range(3):
                        r = (3 * i + j) * D1
                        for s, n, dst in ((0, i, qst), (1, j, kst)):
                            src = qk_parts[s, n].rearrange("(g h d) t -> d g h t", g=NHG, h=HG)[:, bass.ds(g, 1)]
                            sp.dma_start(dst[r:r + D1, bass.ds(slot, 1)], src).then_inc(stack_in, 16)
                sp.dma_start(qst[ROWS:ROWS + 3, bass.ds(slot, 1)],
                             a["c_zeros"].rearrange("r (s h t) -> r s h t", s=1, h=HG)).then_inc(stack_in, 16)

            def maxima(g, slot):
                sp.wait_ge(mpart_ready, g + 1)
                sp.dma_start(max_parts[bass.ds(g, 1)].rearrange("g i m q -> m (g i) q"),
                             mpart[0:HG * NT]).then_inc(max_out, 16)
                sp.wait_ge(max_out, 16 * (g + 1))
                sp.dma_start(qst[ROWS:ROWS + 3, bass.ds(slot, 1)],
                             max_parts[bass.ds(g, 1)].rearrange("g i (h t) q -> i g h (t q)", h=HG)).then_inc(max_in, 16)

            for s in range(2):
                sp.wait_ge(stack_clear, 2 * (s + 1))
                sp.dma_start(kst[ROWS:ROWS + 3, s], a["c_ones"].rearrange("r (h t) -> r h t", h=HG)).then_inc(ones_in, 16)
                stack(s, s)
                sp.wait_ge(ones_in, 16 * (s + 1))
                sp.wait_ge(stack_in, 16 * NSTACK * (s + 1))
            weights(sp, 0, 0)
            weights_v(sp, 0)
            sp.wait_ge(w_loaded, 16 * NW)
            weights(sp, 1, 1)
            maxima(0, 0)
            with sp.Fori(1, NHG - 1) as g:
                maxima(g, g % 2)
                sp.wait_ge(pv_done, NS * g)
                stack(g + 1, (g + 1) % 2)
            maxima(NHG - 1, (NHG - 1) % 2)
            with sp.Fori(1, L - 1) as l:
                sp.wait_ge(v_proj, WPT * NT * l)
                weights_v(sp, l)
                sp.wait_ge(w2_ready, NT * l)
                sp.wait_ge(x_done, NT * (l + 1))
                weights(sp, l + 1, (l + 1) % 2)
            sp.wait_ge(v_proj, WPT * NT * (L - 1))
            weights_v(sp, L - 1)
            sp.wait_ge(all_done, 1)
            sp.dma_start(out.rearrange("b (t p) c -> p (b t) c", p=P), x[:, :, :]).then_inc(out_done, 16)
            sp.wait_ge(out_done, 16)

        @block.gpsimd
        def _(gp):
            gp.dma_start(ident[:, :], a["c_ident"]).then_inc(ident_in, 16)
            for dst, n in ((rot[:, :, :], "rot"), (back[:, :], "back"), (centre[:, :], "centre"), (mean[:, :], "mean"),
                           (pattern[:, :], "pattern"), (select[:, :, :], "select"), (carry[:, :], "carry"),
                           (trik, "tri_k"), (triq, "tri_q")):
                gp.dma_start(dst, a[f"c_{n}"]).then_inc(const_in, 16)
            with nc.allow_non_contiguous_dma(reason="a column a layer"):
                gp.dma_start(ln_g[:, :], a["L0_ffn_ln_g"].rearrange("l c -> c l")).then_inc(const_in, 16)
                gp.dma_start(ln_b[:, :], a["L0_ffn_ln_b"].rearrange("l c -> c l")).then_inc(const_in, 16)
            for i, n in enumerate(("q_scale", "k_scale")):
                gp.dma_start(qks[:, i], a[f"L0_ffn_{n}"].partition_broadcast(P)).then_inc(const_in, 16)

            gp.memset(arena[64:P, 0:4096], 0.0).then_inc(stack_clear, 1)
            gp.memset(arena[64:P, 8192:12288], 0.0).then_inc(stack_clear, 1)
            gp.wait_ge(parts_out, 96)
            gp.wait_ge(v_ready, 4)
            gp.memset(arena[64:P, 4096:8192], 0.0).then_inc(stack_clear, 1)
            gp.memset(arena[64:P, 12288:16384], 0.0).then_inc(stack_clear, 1)

            def it(n, A, B, F, G):
                if A:
                    gp.wait_ge(rot_ready, 2 * n)
                    for s in range(2):
                        gp.wait_ge(qkn_ready, 2 * n + s + 1)
                        for o, i in ((0, DH // 2), (DH // 2, 0)):
                            gp.tensor_tensor(rots[:, s, :, o:o + DH // 2], qkn[:, s, :, i:i + DH // 2],
                                             tab(n // NT, s, 1)[:, :, o:o + DH // 2].to_broadcast([P, H, DH // 2]),
                                             ALU.mult).then_inc(sin_ready, 1)

            flat(gp, it)

        @block.scalar
        def _(act):
            def norm_sqrt(i):
                act.wait_ge(sumsq_ready, i + 1)
                act.activation(stat[:, 5, :], stat[:, 4, :], ACT.Sqrt).then_inc(sqrt_ready, 1)

            norm_sqrt(0)
            for b in range(4):
                act.wait_ge(xnT_ready, b + 1)
                act.activation(xnT[:, 512 * b:512 * b + 512], bank[:, b, :], ACT.Copy).then_inc(xnT_read, 1)
            act.wait_ge(w_in_in, 128)
            for s in range(2):
                if s:
                    act.wait_ge(parts_ready, 3)
                for b in range(4):
                    act.wait_ge(qk_ready, 4 * s + b + 1)
                    act.activation(raw[:, 512 * b:512 * b + 512], bank[:, (4 - 4 * s) + b, :], ACT.Identity,
                                   bias=b_qk[:, s:s + 1]).then_inc(qk_read, 1)

            def exps(k):
                for s, (qc, kt) in enumerate(steps):
                    lo = first_query(qc, kt)
                    for h in range(HG):
                        u = HG * s + h
                        act.wait_ge(score_ready, HG * NS * k + u + 1)
                        if h == 0:
                            act.wait_ge(pv_done, NS * k + (s - 1 if s >= 2 else 0))
                        act.activation(ring[:, u % 8, lo:QC], bank[:, 4 + u % 3, lo:QC], ACT.Exp,
                                       scale=SCALE1).then_inc(exp_done, 1)

            exps(0)
            with act.Fori(1, NHG) as k:
                exps(k)
            for b in range(4):
                act.wait_ge(yT_ready, b + 1)
                act.activation(y1T[:, 512 * b:512 * b + 512], bank[:, b, :], ACT.Copy).then_inc(yT_read, 1)
            norm_sqrt(1)
            norm_sqrt(2)

            def it(n, A, B, F, G):
                k = n - 2

                def squares(half):
                    act.wait_ge(qk_proj, 2 * n + half + 1)
                    act.wait_ge(rot_ready, 2 * n)
                    act.activation(sq[:, H * DH * half:H * DH * (half + 1)],
                                   bank[:, 2 * half:2 * half + 2, :].rearrange("p b n -> p (b n)"), ACT.Square).then_inc(qk_sq, 1)

                def turned(half):
                    for b in (2 * half, 2 * half + 1):
                        act.wait_ge(qkT_ready, 4 * n + b + 1)
                        dst = qT[:, 4 * b:4 * b + 4, :] if b < 2 else kT[:, 4 * b - 8:4 * b - 4, W:W + P]
                        act.activation(dst, bank[:, b, :].rearrange("p (k t) -> p k t", k=4), ACT.Copy).then_inc(qkT_read, 1)

                if A:
                    squares(0)
                if B:
                    act.wait_ge(s_sub, n)
                    act.activation(prob[:, :, :, :], prob[:, :, :, :], ACT.Exp).then_inc(s_exp, 1)
                if G:
                    act.wait_ge(hT_ready, k)
                    act.wait_ge(w2_ready, k - 1)
                    act.activation(hT[:, 0:2, :], bank[:, 7, 0:2 * P].rearrange("p (k t) -> p k t", k=2),
                                   ACT.Copy).then_inc(hT_read, 1)
                    act.activation(hT[0:FF - 2 * P, 2, :], bank[0:FF - 2 * P, 7, 2 * P:3 * P], ACT.Copy).then_inc(hT_read, 1)
                if F:
                    act.wait_ge(xc_read, k + 1)
                    act.wait_ge(var_ready, k)
                    act.activation(xsq[:, :], xc[:, :], ACT.Square).then_inc(xsq_ready, 1)
                if A:
                    squares(1)
                    act.wait_ge(back_ready, n + 1)
                    act.wait_ge(s_ready, n)
                    act.activation(kT[:, :, 0:W], bank[:, 6, 0:8 * W].rearrange("p (k t) -> p k t", k=8),
                                   ACT.Copy).then_inc(back_read, 1)
                if A:
                    act.wait_ge(rn_ready, n)
                    act.wait_ge(ss_ready, n + 1)
                    act.activation(rt[:, :], ss[:, :], ACT.Sqrt).then_inc(rt_ready, 1)
                if F:
                    act.wait_ge(var_read, k + 1)
                    act.wait_ge(rstd_ready, k)
                    act.activation(dev[:, :], var[:, :], ACT.Sqrt).then_inc(dev_ready, 1)
                if B:
                    for i in range(2):
                        act.wait_ge(pT_ready, 2 * (n - 1) + i + 1)
                        act.wait_ge(pv_ready, n - 1)
                        act.activation(probT[:, 4 * i:4 * i + 4, :], bank[:, 4 + i, :].rearrange("p (k t) -> p k t", k=4),
                                       ACT.Copy).then_inc(pT_read, 1)
                if A:
                    for j in range(WPT):
                        act.wait_ge(v_proj, 4 * n + j + 1)
                        act.wait_ge(pv_ready, n)
                        act.activation(vv[:, j], bank[:, 6 + j % 2, :].rearrange("p (k d) -> p k d", k=8),
                                       ACT.Copy).then_inc(v_read, 1)
                    turned(0)
                if B:
                    for i in range(2):
                        act.wait_ge(attT_ready, 2 * (n - 1) + i + 1)
                        act.wait_ge(wo_ready, n - 1)
                        act.activation(attT[:, 4 * i:4 * i + 4, :], bank[:, 4 + i, :].rearrange("p (k t) -> p k t", k=4),
                                       ACT.Copy).then_inc(attT_read, 1)
                if A:
                    turned(1)
                if F:
                    act.wait_ge(hh_ready, k)
                    act.wait_ge(h_read, k + 1)
                    act.activation(gg[:, :], hg[:, FF:2 * FF], ACT.Gelu).then_inc(gelu_ready, 1)
                if A:
                    act.activation(fetch[:, :], carry[:, 0:1], ACT.Exp)

            flat(act, it)
            norm_sqrt(3)

        @block.tensor
        def _(pe):
            mm = pe.matmul
            pe.wait_ge(ident_in, 16)
            for t in range(NT):
                if t == 0:
                    pe.wait_ge(xn_ready, 1)
                last = pe.transpose(bank[:, t // 4, P * (t % 4):P * (t % 4) + P], xn[:, t, :], ident[:, :])
                if t % 4 == 3:
                    last.then_inc(xnT_ready, 1)
            pe.wait_ge(w_in_in, 128)
            for s in range(2):
                for b in range(4):
                    pe.wait_ge(xnT_read, b + 1)
                    mm(bank[:, 4 - 4 * s + b, :], w_in[:, s, :], xnT[:, 512 * b:512 * b + 512],
                       start=True, stop=True).then_inc(qk_ready, 1)
            for t in range(NT):
                pe.wait_ge(qk_read, t // 4 + 1)
                last = mm(bank[:, 4 + t // 4, P * (t % 4):P * (t % 4) + P], xnT[:, P * t:P * t + P], w_in[:, 2, :],
                          start=True, stop=True)
                if t % 4 == 3:
                    last.then_inc(v_ready, 1)

            def scores_for_max(k, slot, i):
                h, t, c = pieces[i]
                pe.wait_ge(piece_read, NPC * k + (i - 1 if i >= 2 else 0))
                if i == 0:
                    pe.wait_ge(mpart_ready, k)
                keys = P * (t + 1)
                lo, hi = 1024 * c, min(keys, 1024 * (c + 1))
                for j in range(lo, hi, 512):
                    n = min(512, hi - j)
                    b = 2 * (i % 2) + (j - lo) // 512
                    diagonal = j + n == keys
                    last = mm(bank[:, b, 0:n], qst[:, bass.ds(slot, 1), h, P * t:P * t + P],
                              kst[:, bass.ds(slot, 1), h, j:j + n], start=True, stop=True)
                    if diagonal:
                        last = mm(bank[:, b, n - P:n], identb[:, :], triq, start=False, stop=True, skip_group_check=True)
                last.then_inc(piece_ready, 1)

            def turn_maxima(k):
                pe.wait_ge(negm_ready, k + 1)
                pe.transpose(bank[:, 0, 0:P], negm, ident[:, :]).then_inc(negmT_ready, 1)

            def scores(k, slot, s):
                qc, kt = steps[s]
                lo = first_query(qc, kt)
                if s == 0:
                    pe.wait_ge(max_in, 16 * (k + 1))
                for h in range(HG):
                    u = HG * s + h
                    b = 4 + u % 3
                    pe.wait_ge(exp_done, HG * NS * k + (u - 2 if u >= 3 else 0))
                    r = kt - QC // P * qc
                    last = mm(bank[:, b, lo:QC], kst[:, bass.ds(slot, 1), h, P * kt:P * kt + P],
                              qst[:, bass.ds(slot, 1), h, QC * qc + lo:QC * qc + QC], start=True, stop=True)
                    if r >= 0:
                        hi = P * (r + 1)
                        last = mm(bank[:, b, lo:hi], identb[:, :], trik[:, QC - hi + lo:QC], start=False, stop=True,
                                  skip_group_check=True)
                    last.then_inc(score_ready, 1)

            def values(k, s):
                qc, kt = steps[s]
                lo = first_query(qc, kt)
                pe.wait_ge(exp_done, HG * NS * k + HG * (s + 1))
                if s == 0:
                    pe.wait_ge(vcur_ready, k + 1)
                if kt == 0:
                    pe.wait_ge(oT_read, NQC * k + qc)
                for h in range(HG):
                    last = mm(bank[32 * h:32 * h + D1 + 1, 7, lo:QC], vcur[:, kt, h, :], ring[:, (HG * s + h) % 8, lo:QC],
                              start=kt == 0, stop=True, skip_group_check=True)
                last.then_inc(pv_done, 1)

            def turn_output(k, qc):
                pe.wait_ge(o_read, NQC * k + qc + 1)
                for i in range(4):
                    last = pe.transpose(bank[:, 7, P * i:P * i + P], o_sb[:, P * i:P * i + P], ident[:, :])
                last.then_inc(oT_ready, 1)

            def group(k, slot, other, more):
                for what, *i in order:
                    if what == "score":
                        scores(k, slot, i[0])
                    elif what == "pv":
                        values(k, i[0])
                    elif what == "out":
                        turn_output(k, i[0])
                    elif more:
                        scores_for_max(k + 1, other, i[0])
                if more:
                    turn_maxima(k + 1)

            pe.wait_ge(identb_ready, 1)
            pe.wait_ge(vaug_ready, 5)
            pe.wait_ge(const_in, 16 * NCONST)
            pe.wait_ge(ones_in, 16)
            pe.wait_ge(stack_in, 16 * NSTACK)
            for i in range(NPC):
                scores_for_max(0, 0, i)
            turn_maxima(0)
            pe.wait_ge(ones_in, 32)
            pe.wait_ge(stack_in, 16 * NSTACK * 2)
            group(0, 0, 1, True)
            with pe.Fori(1, NHG - 1) as k:
                pe.wait_ge(stack_in, 16 * NSTACK * (k + 2))
                group(k, k % 2, (k + 1) % 2, True)
            group(NHG - 1, (NHG - 1) % 2, NHG % 2, False)

            pe.wait_ge(oT_read, NHG * NQC)
            for t in range(NT):
                last = pe.transpose(bank[:, t // 4, P * (t % 4):P * (t % 4) + P], kept[:, t, :], ident[:, :])
                if t % 4 == 3:
                    last.then_inc(yT_ready, 1)
            for t in range(NT):
                pe.wait_ge(yT_read, t // 4 + 1)
                last = mm(bank[:, 4 + t // 4, P * (t % 4):P * (t % 4) + P], y1T[:, P * t:P * t + P], w_in[:, 3, :],
                          start=True, stop=True)
                if t % 4 == 3:
                    last.then_inc(z_ready, 1)

            def it(n, A, B, F, G):
                wa, wb, wf, wg = ((n - d) // NT % 2 if on else None for d, on in enumerate((A, B, F, G)))
                k = n - 2

                def project(half):
                    for b in (2 * half, 2 * half + 1):
                        last = mm(bank[:, b, :], xsT[:, W:W + P],
                                  wqk[:, bass.ds(wa, 1), 512 * b:512 * b + 512], start=True, stop=True)
                    last.then_inc(qk_proj, 1)

                def turn_qk(half):
                    pe.wait_ge(rot_ready, 2 * n + half + 1)
                    for i in range(8 * half, 8 * half + 8):
                        src = qkn[:, i // 8, 2 * (i % 8):2 * (i % 8) + 2, :].rearrange("p h d -> p (h d)")
                        last = pe.transpose(bank[:, i // 4, P * (i % 4):P * (i % 4) + P], src, ident[:, :])
                        if i % 4 == 3:
                            last.then_inc(qkT_ready, 1)

                def value_projection(j):
                    wv2 = wv[:, :].rearrange("p (k h d) -> p k h d", h=2, d=DH)
                    if j == 0:
                        pe.wait_ge(wv_loaded, 16 * (n // NT + 1))
                        pe.wait_ge(back_read, n + 1)
                    elif j == 1 and F:
                        pe.wait_ge(var_read, k + 1)
                    elif j >= 2:
                        pe.wait_ge(v_read, 4 * n + j - 1)
                    for odd in range(2):
                        if j == 1 and odd == 1 and B:
                            pe.wait_ge(pT_read, 2 * n)
                        last = mm(bank[DH * odd:DH * odd + DH, 6 + j % 2, :], xsT[:, W * j:W * j + 2 * W], wv2[:, :, odd, :],
                                  start=True, stop=True)
                    last.then_inc(v_proj, 1)

                def project_output(half):
                    pe.wait_ge(attT_read, 2 * (n - 1) + half + 1)
                    for i in range(4 * half, 4 * half + 4):
                        last = mm(bank[:, 0, 0:P], attT[:, i, :], wo[:, bass.ds(wb, 1), i, :], start=i == 0, stop=i == 7,
                                  skip_group_check=True)
                    if half:
                        last.then_inc(wo_ready, 1)

                if F:
                    pe.wait_ge(xmT_read, k + 1)
                    mm(bank[:, 6, 0:P], centre[:, :], xmT[:, 0:P], start=True, stop=True).then_inc(xc_ready, 1)
                if A:
                    pe.wait_ge(xs_ready, n + 1)
                    pe.wait_ge(qkT_read, 4 * n)
                    pe.wait_ge(w_loaded, 16 * NW * (n // NT + 1))
                    project(0)
                if G:
                    pe.wait_ge(hh_ready, k)
                    for i in range(3):
                        m = min(P, FF - P * i)
                        last = pe.transpose(bank[0:m, 7, P * i:P * i + P], gated[:, P * i:P * i + m], ident[:, :])
                    last.then_inc(hT_ready, 1)
                if A:
                    project(1)
                    if F:
                        pe.wait_ge(xc_read, k + 1)
                    elif n == 0:
                        pe.wait_ge(carry_zero, 1)
                    else:
                        pe.wait_ge(v_read, 4 * n)
                    mm(bank[:, 6, 0:8 * W], back[:, :], kT[:, :, P:P + W], start=True, stop=True).then_inc(back_ready, 1)
                if G:
                    pe.wait_ge(hT_read, 2 * k)
                    for i in range(3):
                        m = min(P, FF - P * i)
                        last = mm(bank[:, 7, 3 * P:4 * P], hT[0:m, i, :], w2[0:m, bass.ds(wg, 1), i, :], start=i == 0, stop=i == 2)
                    last.then_inc(w2_ready, 1)
                if B:
                    pe.wait_ge(s_exp, n)
                    for i in range(8):
                        last = pe.transpose(bank[:, 4 + i // 4, P * (i % 4):P * (i % 4) + P],
                                            prob[:, i].rearrange("p h c -> p (h c)"), ident[:, :])
                        if i % 4 == 3:
                            last.then_inc(pT_ready, 1)
                if F:
                    pe.wait_ge(xsq_ready, k + 1)
                    pe.wait_ge(x_done, NT + k)
                    mm(bank[:, 7, 0:P], mean[:, :], xsq[:, :], start=True, stop=True).then_inc(var_ready, 1)
                if A:
                    value_projection(0)
                    value_projection(1)
                elif B:
                    pe.wait_ge(pT_read, 2 * n)
                if B:
                    for i in range(8):
                        for j in range(WPT):
                            for odd in range(2):
                                r = DH * odd
                                last = mm(bank[W * j:W * j + W, 4 + odd, DH * i:DH * i + DH], probT[r:r + DH, i, W * j:W * j + W],
                                          vv[r:r + DH, j, i, :], start=True, stop=True)
                    last.then_inc(pv_ready, 1)
                if A:
                    value_projection(2)
                    value_projection(3)
                if A:
                    turn_qk(0)
                if B:
                    pe.wait_ge(att_ready, n)
                    for i in range(8):
                        last = pe.transpose(bank[:, 4 + i // 4, P * (i % 4):P * (i % 4) + P],
                                            att[:, i].rearrange("p h d -> p (h d)"), ident[:, :])
                        if i % 4 == 3:
                            last.then_inc(attT_ready, 1)
                if B:
                    if A:
                        pe.wait_ge(qkT_read, 4 * n + 1)
                    project_output(0)
                if A:
                    turn_qk(1)
                if B:
                    project_output(1)
                if A:
                    pe.wait_ge(xcur_ready, n + 2)
                    pe.wait_ge(qkT_read, 4 * n + 2)
                    pe.transpose(bank[:, 1, 0:P], xcur[:, :], ident[:, :]).then_inc(xT_ready, 1)
                if F:
                    pe.wait_ge(xnf_ready, k + 1)
                    if A:
                        pe.wait_ge(v_read, 4 * n + 4)
                    else:
                        pe.wait_ge(var_read, k + 1)
                    for i in range(2):
                        last = mm(bank[:, 6 + i, 0:FF], xcg[:, :], w1[:, bass.ds(wf, 1), FF * i:FF * i + FF],
                                  start=True, stop=True)
                    last.then_inc(h_ready, 1)
                if B:
                    pe.wait_ge(xm_ready, n)
                    pe.transpose(bank[:, 0, P:2 * P], xm[:, :], ident[:, :]).then_inc(xmT_ready, 1)
                if A:
                    if B:
                        pe.wait_ge(attT_read, 2 * n)
                    pe.wait_ge(back_read, n + 1)
                    pe.wait_ge(qkT_read, 4 * n + 4)
                    if isinstance(n, int) and n == 0:
                        pe.wait_ge(pattern_ready, 1)
                    for odd in range(2):
                        mm(bank[:, 4 + odd, :], select[:, bass.ds(n % NT, 1), :], pattern8[:, :, :], start=True, stop=True)
                    for i in range(8):
                        for j in range(WPT):
                            for odd in range(2):
                                r = DH * odd
                                last = mm(bank[W * j:W * j + W, 4 + odd, 2 * W * i:2 * W * i + 2 * W],
                                          qT[r:r + DH, i, W * j:W * j + W], kT[r:r + DH, i, W * j:W * j + 2 * W],
                                          start=False, stop=True, skip_group_check=True)
                    last.then_inc(s_ready, 1)
            pe.wait_ge(xcur_ready, 1)
            pe.wait_ge(z_read, 4)
            pe.transpose(bank[:, 1, 0:P], xcur[:, :], ident[:, :]).then_inc(xT_ready, 1)
            flat(pe, it)

        @block.vector
        def _(ve):
            count = [0]

            def step(ins):
                count[0] += 1
                ins.then_inc(vec_step, 1)
                ve.wait_ge(vec_step, count[0])

            def over(s, n):
                return stat[:, s, :].unsqueeze(2).to_broadcast([P, NT, n])

            def norm(i, src, dst, work):
                step(ve.tensor_reduce(stat[:, 0, :], src, AX.X, ALU.add))
                step(ve.tensor_scalar(stat[:, 1, :], stat[:, 0, :], -1.0 / C, None, ALU.mult))
                step(ve.tensor_tensor(dst, src, over(1, C), ALU.add))
                step(ve.tensor_tensor(work, dst, dst, ALU.mult))
                step(ve.tensor_reduce(stat[:, 3, :], work, AX.X, ALU.add))
                ve.tensor_scalar(stat[:, 4, :], stat[:, 3, :], 1.0 / C, EPS, ALU.mult, ALU.add).then_inc(sumsq_ready, 1)
                ve.wait_ge(sqrt_ready, i + 1)
                step(ve.reciprocal(stat[:, 4, :], stat[:, 5, :]))

            ve.wait_ge(x_in, 16)
            norm(0, x[:, :, :], xn, raw.rearrange("p (t c) -> p t c", t=NT))
            ve.tensor_tensor(xn, xn, over(4, C), ALU.mult).then_inc(xn_ready, 1)
            ve.wait_ge(ident_in, 16)
            ve.tensor_copy(identb[:, :], ident[:, :]).then_inc(identb_ready, 1)
            step(ve.memset(vaug[:, :, :, D1:D1 + 1], 1.0))
            step(ve.memset(pmax, NEG))
            step(ve.memset(negm, 0.0))
            ve.wait_ge(const_in, 16 * NCONST)
            half = DH // 2
            for s in range(2):
                for cs, o, i, m in ((0, 0, 0, DH), (1, 0, half, half), (1, half, 0, half)):
                    step(ve.tensor_tensor(table[:, :, s, cs, o:o + m], qks[:, s, :, i:i + m],
                                          rot[:, 2 * s + cs:2 * s + cs + 1, o:o + m].to_broadcast([P, L, m]), ALU.mult))
            ve.tensor_copy(pattern8[:, :, :], pattern[:, :].unsqueeze(1).to_broadcast([P, 8, 2 * W])).then_inc(pattern_ready, 1)
            for s, p3 in ((0, parts_q), (1, parts_k)):
                ve.wait_ge(qk_read, 4 * (s + 1))
                for i in range(3):
                    ve.tensor_copy(p3[i], raw).then_inc(parts_ready, 1)
                    if i < 2:
                        ve.wait_ge(parts_ready, 3 * s + i + 1)
                        step(ve.tensor_tensor(raw, raw, p3[i], ALU.subtract))
            ve.wait_ge(w_in_in, 128)
            for b in range(4):
                ve.wait_ge(v_ready, b + 1)
                bias = b_vo[:, 0:1, :].rearrange("p o (h d) -> p o h d", h=H1).to_broadcast([P, 4, H1, D1])
                ve.tensor_tensor(vaug[:, 4 * b:4 * b + 4, :, 0:D1],
                                 bank[:, 4 + b, :].rearrange("p (t h d) -> p t h d", t=4, h=H1), bias, ALU.add).then_inc(vaug_ready, 1)
            ve.wait_ge(vaug_ready, 4)
            ve.memset(bank[:, 7, :], 0.0).then_inc(vaug_ready, 1)
            ve.wait_ge(vaug_ready, 5)

            def max_piece(k, i):
                h, t, c = pieces[i]
                n = min(P * (t + 1) - 1024 * c, 1024)
                ve.wait_ge(piece_ready, NPC * k + i + 1)
                src = bank[:, 2 * (i % 2):2 * (i % 2) + 2, :].rearrange("p b n -> p (b n)")[:, 0:n]
                ve.tensor_reduce(pmax[:, h * NT + t, c:c + 1], src, AX.X, ALU.max).then_inc(piece_read, 1)

            def split_maxima(k):
                ve.wait_ge(piece_read, NPC * (k + 1))
                m = negm[:, 0:HG * NT]
                ve.tensor_reduce(m, pmax, AX.X, ALU.max).then_inc(max_step, 1)
                ve.wait_ge(max_step, 5 * k + 1)
                ve.tensor_scalar(m, m, -1.0, None, ALU.mult).then_inc(negm_ready, 1)
                ve.wait_ge(negmT_ready, k + 1)
                ve.wait_ge(max_out, 16 * k)
                ve.tensor_copy(mpart[:, 0, :], bank[:, 0, 0:P]).then_inc(max_step, 1)
                ve.wait_ge(max_step, 5 * k + 2)
                ve.tensor_tensor(mrest, bank[:, 0, 0:P], mpart[:, 0, :], ALU.subtract).then_inc(max_step, 1)
                ve.wait_ge(max_step, 5 * k + 3)
                ve.tensor_copy(mpart[:, 1, :], mrest).then_inc(max_step, 1)
                ve.wait_ge(max_step, 5 * k + 4)
                ve.tensor_tensor(mrest, mrest, mpart[:, 1, :], ALU.subtract).then_inc(max_step, 1)
                ve.wait_ge(max_step, 5 * k + 5)
                ve.tensor_copy(mpart[:, 2, :], mrest).then_inc(mpart_ready, 1)

            y = kept[:, :, :].rearrange("p t (g h d) -> p t g h d", g=NHG, h=HG)

            def group(k, more):
                ve.wait_ge(pv_done, NS * k)
                ve.tensor_copy(vcur, vaug[:, :, bass.ds(HG * k, HG), :]).then_inc(vcur_ready, 1)
                for what, *i in order:
                    if what == "pv":
                        qc, kt = steps[i[0]]
                        if kt == QC // P * (qc + 1) - 1:
                            ve.wait_ge(pv_done, NS * k + i[0] + 1)
                            ve.wait_ge(oT_ready, NQC * k + qc)
                            ve.tensor_copy(o_sb, bank[:, 7, :]).then_inc(o_read, 1)
                    elif what == "out":
                        qc = i[0]
                        o = bank[:, 7, :].rearrange("p (t h d) -> p t h d", t=4, h=HG)
                        r = rden.rearrange("p (t h o) -> p t h o", t=4, h=HG)
                        ve.wait_ge(oT_ready, NQC * k + qc + 1)
                        ve.wait_ge(oT_read, NQC * k + qc)
                        ve.reciprocal(r, o[:, :, :, D1:D1 + 1]).then_inc(den_ready, 1)
                        ve.wait_ge(den_ready, NQC * k + qc + 1)
                        dst = y[:, 4 * qc:4 * qc + 4, bass.ds(k, 1), :, :].rearrange("p t g h d -> p t (g h) d")
                        ve.tensor_tensor(dst, o[:, :, :, 0:D1], r.to_broadcast([P, 4, HG, D1]), ALU.mult).then_inc(oT_read, 1)
                    elif what == "max" and more:
                        max_piece(k + 1, i[0])
                if more:
                    split_maxima(k + 1)

            for i in range(NPC):
                max_piece(0, i)
            split_maxima(0)
            group(0, True)
            with ve.Fori(1, NHG - 1) as k:
                group(k, True)
            group(NHG - 1, False)

            for b in range(4):
                ve.wait_ge(z_ready, b + 1)
                ve.tensor_tensor(z[:, 4 * b:4 * b + 4, :], bank[:, 4 + b, :].rearrange("p (t c) -> p t c", t=4),
                                 b_vo[:, 1:2, :].to_broadcast([P, 4, C]), ALU.add).then_inc(z_read, 1)
            ve.wait_ge(z_read, 4)
            norm(1, z, z, zsq)
            step(ve.tensor_tensor(z, z, over(4, C), ALU.mult))
            step(ve.tensor_tensor(kept[:, :, :], x[:, :, :], z, ALU.add))
            norm(2, kept[:, :, :], x[:, :, :], zsq)
            for t in range(NT):
                ve.tensor_scalar(x[:, t, :], x[:, t, :], stat[:, 4, t:t + 1], None, ALU.mult).then_inc(x_done, 1)

            ve.wait_ge(x_done, NT)
            step(ve.memset(kT, 0.0))
            step(ve.memset(xsT, 0.0))
            step(ve.memset(xmT, 0.0))
            ve.memset(gated[:, :], 0.0).then_inc(carry_zero, 1)
            ve.wait_ge(carry_zero, 1)

            def x_copy(n):
                ve.wait_ge(x_done, n + 1)
                ve.wait_ge(xT_ready, n)
                ve.tensor_copy(xcur[:, :], x[:, bass.ds(n % NT, 1), :].rearrange("p o c -> p (o c)")).then_inc(xcur_ready, 1)

            def x_shift(n):
                ve.tensor_scalar(xsT[:, 0:W + 1], xsT[:, P:P + W + 1], carry[:, bass.ds(n % NT, 1)], None,
                                 ALU.mult).then_inc(x_step, 1)
                ve.wait_ge(x_step, n + 1)
                ve.wait_ge(xT_ready, n + 1)
                ve.tensor_copy(xsT[0:64, W:W + P], bank[0:64, 1, 0:P]).then_inc(x_low, 1)
                ve.wait_ge(x_low, n + 1)
                ve.tensor_copy(xsT[64:P, W + 1:W + P + 1], bank[64:P, 1, 0:P]).then_inc(xs_ready, 1)

            def it(n, A, B, F, G):
                wb, wf = ((n - d) // NT % 2 if on else None for d, on in ((1, B), (2, F)))
                k = n - 2
                tb, tg = (bass.ds((n - d) % NT, 1) if on else None for d, on in ((1, B), (3, G)))
                flatten = lambda v: v.rearrange("p o c -> p (o c)")
                p4 = prob.rearrange("p k h c -> p h k c")
                by_head = lambda v: v.rearrange("p (h k) -> p h k", h=2)
                sq4 = sq.rearrange("p (s h d) -> p s h d", s=2, h=H)

                def sum_squares(s):
                    ve.wait_ge(qk_sq, 2 * n + s + 1)
                    ve.wait_ge(rt_ready, n)
                    ve.tensor_reduce(ss[:, H * s:H * s + H], sq4[:, s], AX.X, ALU.add).then_inc(ss_step, 1)

                def cosine_half(s):
                    ve.wait_ge(qkn_ready, 2 * n + s + 1)
                    ve.tensor_tensor(sq4[:, s], qkn[:, s], tab(n // NT, s, 0).to_broadcast([P, H, DH]), ALU.mult).then_inc(cos_ready, 1)

                def rotated(s):
                    ve.wait_ge(cos_ready, 2 * n + s + 1)
                    ve.wait_ge(sin_ready, 4 * n + 2 * (s + 1))
                    ve.tensor_tensor(qkn[:, s], sq4[:, s], rots[:, s], ALU.add).then_inc(rot_ready, 1)

                if F:
                    ve.wait_ge(xc_ready, k + 1)
                    ve.wait_ge(xnf_ready, k)
                    ve.wait_ge(xsq_ready, k)
                    ve.tensor_copy(xc[:, :], bank[:, 6, 0:P]).then_inc(xc_read, 1)
                if A:
                    x_copy(n + 1)
                    sum_squares(0)
                if G:
                    ve.wait_ge(w2_ready, k)
                    ve.wait_ge(xb_ready, k)
                    ve.tensor_tensor(flatten(x[:, tg, :]), bank[:, 7, 3 * P:4 * P], flatten(x[:, tg, :]), ALU.add).then_inc(x_done, 1)
                if A:
                    sum_squares(1)
                    ve.wait_ge(ss_step, 2 * (n + 1))
                    ve.tensor_scalar(ss[:, :], ss[:, :], 1e-24, None, ALU.max).then_inc(ss_ready, 1)
                if F:
                    ve.wait_ge(var_ready, k + 1)
                    ve.wait_ge(dev_ready, k)
                    ve.tensor_scalar(var[:, :], bank[:, 7, 0:P], EPS, None, ALU.add).then_inc(var_read, 1)
                if B:
                    ve.wait_ge(s_exp, n)
                    ve.tensor_reduce(by_head(ssum), p4, AX.X, ALU.add).then_inc(s_sum, 1)
                    ve.wait_ge(s_sum, n)
                    ve.wait_ge(att_ready, n - 1)
                    ve.reciprocal(rsum[:, :], ssum[:, :]).then_inc(s_rsum, 1)
                if A:
                    ve.wait_ge(rt_ready, n + 1)
                    ve.wait_ge(qkn_ready, 2 * n)
                    ve.reciprocal(rn[:, :], rt[:, :]).then_inc(rn_ready, 1)
                    ve.wait_ge(rn_ready, n + 1)
                    ve.wait_ge(qkT_ready, 4 * n)
                    for s in range(2):
                        ve.tensor_tensor(qkn[:, s], bank[:, 2 * s:2 * s + 2, :].rearrange("p b (h d) -> p (b h) d", d=DH),
                                         rn[:, H * s:H * s + H].unsqueeze(2).to_broadcast([P, H, DH]), ALU.mult).then_inc(qkn_ready, 1)
                    cosine_half(0)
                    rotated(0)
                if B:
                    ve.wait_ge(pv_ready, n)
                    ve.wait_ge(s_rsum, n)
                    ve.wait_ge(attT_ready, 2 * (n - 1))
                    ve.tensor_tensor(att.rearrange("p k h d -> p h k d"), bank[:, 4:6, :].rearrange("p b (k d) -> p b k d", d=DH),
                                     by_head(rsum).unsqueeze(3).to_broadcast([P, 2, 8, DH]), ALU.mult).then_inc(att_ready, 1)
                if A:
                    cosine_half(1)
                    rotated(1)
                if F:
                    ve.wait_ge(dev_ready, k + 1)
                    ve.wait_ge(xnf_ready, k)
                    ve.reciprocal(rstd[:, :], dev[:, :]).then_inc(rstd_ready, 1)
                    ve.wait_ge(rstd_ready, k + 1)
                    ve.wait_ge(h_ready, k)
                    ln = bass.ds(k // NT, 1)
                    ve.scalar_tensor_tensor(out=xcg[:, :], in0=xc[:, :], scalar=ln_g[:, ln], in1=rstd[:, :], op0=ALU.mult,
                                            op1=ALU.mult).then_inc(ln_step, 1)
                    ve.wait_ge(ln_step, k + 1)
                    ve.tensor_scalar(xcg[:, :], xcg[:, :], ln_b[:, ln], None, ALU.add).then_inc(xnf_ready, 1)
                if A:
                    ve.wait_ge(v_proj, 4 * n + 4)
                    x_shift(n + 1)
                if B:
                    ve.wait_ge(wo_ready, n)
                    ve.wait_ge(xmT_ready, n - 1)
                    ve.tensor_tensor(xm[:, :], bank[:, 0, 0:P], flatten(x[:, tb, :]), ALU.add).then_inc(xm_ready, 1)
                if F:
                    ve.wait_ge(h_ready, k + 1)
                    ve.wait_ge(hh_ready, k)
                    ve.tensor_tensor(hg.rearrange("p (i f) -> p i f", i=2), bank[:, 6:8, 0:FF],
                                     b1[:, bass.ds(wf, 1), :].rearrange("p o (i f) -> p (o i) f", i=2), ALU.add).then_inc(h_read, 1)
                if B:
                    ve.wait_ge(xm_ready, n)
                    ve.tensor_tensor(flatten(x[:, tb, :]), xm[:, :], flatten(b2[:, bass.ds(wb, 1), :]), ALU.add).then_inc(xb_ready, 1)
                if B:
                    ve.wait_ge(xc_ready, n - 1)
                    ve.tensor_scalar(xmT[64:P, 0:1], xmT[64:P, P:P + 1], carry[64:P, tb], None, ALU.mult).then_inc(xm_step, 1)
                    ve.wait_ge(xmT_ready, n)
                    ve.tensor_copy(xmT[0:64, 0:P], bank[0:64, 0, P:2 * P]).then_inc(xm_step, 1)
                    ve.wait_ge(xm_step, 2 * n)
                    ve.tensor_copy(xmT[64:P, 1:P + 1], bank[64:P, 0, P:2 * P]).then_inc(xmT_read, 1)
                if F:
                    ve.wait_ge(gelu_ready, k + 1)
                    ve.wait_ge(hT_ready, k)
                    ve.tensor_tensor(gated[:, :], hg[:, 0:FF], gg[:, :], ALU.mult).then_inc(hh_ready, 1)
                if A:
                    ve.wait_ge(s_ready, n + 1)
                    s4 = bank[:, 4:6, :].rearrange("p b (k c) -> p b k c", c=2 * W)
                    if B:
                        ve.wait_ge(s_sub, n)
                    ve.tensor_reduce(by_head(smax), s4, AX.X, ALU.max).then_inc(s_max, 1)
                    ve.wait_ge(s_max, n + 1)
                    ve.wait_ge(pT_ready, 2 * n)
                    ve.wait_ge(s_sum, n)
                    ve.tensor_tensor(p4, s4, by_head(smax).unsqueeze(3).to_broadcast([P, 2, 8, 2 * W]), ALU.subtract).then_inc(s_sub, 1)

            x_copy(0)
            x_shift(0)
            flat(ve, it)

            ve.wait_ge(x_done, NT + NTILE)
            ve.wait_ge(xs_ready, NTILE + 1)
            norm(3, x[:, :, :], z, zsq)
            step(ve.tensor_tensor(z, z, over(4, C), ALU.mult))
            ve.tensor_tensor(x[:, :, :], kept[:, :, :], z, ALU.add).then_inc(all_done, 1)


_INS = ["L0_attn_x"] + [f"L0_attn_{k}{n}" for n in "qkvo" for k in "Wb"] + [
    f"L0_ffn_{n}" for n in ("Wqkv", "q_scale", "k_scale", "Wo", "ln_g", "ln_b", "W1", "b1", "W2", "b2")]


def kernel(**inputs):
    import concourse.bacc as bacc
    from concourse.bass_utils import run_bass_kernel_spmd

    nc = bacc.Bacc("TRN2", target_bir_lowering=False, num_devices=1)
    arrays, aps = {}, {}
    data = {n: np.ascontiguousarray(inputs[n]) for n in _INS} | constants()
    for name, v in data.items():
        arrays[f"in_{name}"] = v
        aps[name] = nc.dram_tensor(f"in_{name}", v.shape, mybir.dt.from_np(v.dtype), kind="ExternalInput").ap()
        if v.dtype == np.uint16:
            aps[name] = aps[name].bitcast(BF16)
    out = nc.dram_tensor("out_0", (1, T, C), F32, kind="ExternalOutput").ap()
    build(nc, aps, out)
    r = run_bass_kernel_spmd(nc, [arrays], core_ids=[0])
    return r.results[0]["out_0"]
```

```python
from contextlib import ExitStack

import numpy as np
import concourse.bass as bass
from concourse import mybir

F32 = mybir.dt.float32
BF16 = mybir.dt.bfloat16
ALU = mybir.AluOpType
ACT = mybir.ActivationFunctionType
AX = mybir.AxisListType

P = 128
T, C = 2048, 128
NT = T // P
EPS = 1e-5
H1, D1 = 16, 8
HG, NHG = 4, 4
NPAIR = 9
ROWS = NPAIR * D1
QC = 512
NQC = T // QC
SCALE1 = 1.0 / float(np.sqrt(np.float32(D1)))
L, H, DH, W = 6, 16, 64, 32
INNER = H * DH
FF = int(C * 4 * 2 / 3)
WPT = P // W
NTILE = L * NT
QK_SCALE = 8.0
NEG = -3.0e38


def constants():
    half = np.arange(0, DH, 2, dtype=np.float64)
    freq = 1.0 / 10000.0 ** (half / DH)
    base = (half + 0.4 * DH) / (1.4 * DH)
    p = np.arange(P)[:, None]
    ang = np.concatenate([p * freq, p * freq], -1)
    grow = base ** (p / (W // 2))
    grow = np.concatenate([grow, grow], -1)
    sign = np.where(np.arange(DH) < DH // 2, -1.0, 1.0)
    rot = np.stack([np.cos(ang) * grow * QK_SCALE, sign * np.sin(ang) * grow * QK_SCALE,
                    np.cos(ang) / grow, sign * np.sin(ang) / grow], 1)
    c, s, g = np.cos(P * freq), np.sin(P * freq), base ** (P / (W // 2))
    back = np.zeros((P, P))
    n = DH // 2
    for h in (0, DH):
        for f in range(n):
            back[h + f, h + f] = c[f] * g[f]
            back[h + n + f, h + f] = s[f] * g[f]
            back[h + n + f, h + n + f] = c[f] * g[f]
            back[h + f, h + n + f] = -s[f] * g[f]
    centre = np.eye(P) - 1.0 / C
    a = np.arange(W)
    pattern = np.zeros((P, 2 * W))
    pattern[:W, :W] = np.where(a[None, :] < a[:, None], NEG, 0)
    pattern[W:2 * W, :W] = NEG
    pattern[:W, W:] = pattern[W:2 * W, W:] = np.where(a[None, :] > a[:, None], NEG, 0)
    select = np.zeros((P, NT, P))
    for m in range(P):
        select[m % W, :, m] = 1
    for m in range(W):
        select[m, 0, m], select[W + m, 0, m] = 0, 1
    carry = np.ones((P, NT))
    carry[:, 0] = 0
    r = np.arange(P)
    tri_q = np.where(r[None, :] > r[:, None], NEG, 0)
    tri_k = np.zeros((P, QC))
    tri_k[:, :QC - P] = NEG
    tri_k[:, QC - P:] = np.where(r[:, None] > r[None, :], NEG, 0)
    f = lambda x: np.ascontiguousarray(x, dtype=np.float32)
    b = lambda x: np.ascontiguousarray((f(x).view(np.uint32) >> 16).astype(np.uint16))
    return {
        "c_rot": f(rot), "c_back": f(back), "c_centre": f(centre), "c_pattern": b(pattern),
        "c_select": b(select), "c_carry": f(carry), "c_tri_q": b(tri_q), "c_tri_k": b(tri_k),
        "c_ident": f(np.eye(P)), "c_mean": f(np.full((P, P), 1.0 / C)),
        "c_zeros": b(np.zeros((3, HG * T))), "c_ones": b(np.ones((3, HG * T))),
    }


def schedule():
    steps = [(qc, kt) for qc in range(NQC) for kt in range(QC // P * (qc + 1))]
    pieces = [(h, t, c) for h in range(HG) for t in range(NT) for c in range(1 + (t >= NT // 2))]
    order, done = [], 0
    first, last = 6, len(steps) - 4
    for s, (qc, kt) in enumerate(steps):
        want = len(pieces) * min(max(s + 1 - first, 0), last - first) // (last - first)
        products = []
        if s >= 2 and steps[s - 2][0] != steps[s - 1][0]:
            products.append(("out", steps[s - 2][0]))
        if s >= 1:
            products.append(("pv", s - 1))
        scores = [("score", s, h) for h in range(HG)]
        for part in (scores[:2], scores[2:], products):
            order += part
            if done < want:
                order.append(("max", done))
                done += 1
        order += [("max", i) for i in range(done, want)]
        done = max(done, want)
        if want == len(pieces) and ("split", 0) not in order:
            order.append(("split", 0))
    order += [("pv", len(steps) - 1), ("out", NQC - 1)]
    return steps, pieces, order


def build(nc, a, out):
    steps, pieces, order = schedule()
    NS = len(steps)
    NPC = len(pieces)
    nc.disable_value_cache = True
    with ExitStack() as ctx:
        def sb(name, shape, dt=F32):
            return ctx.enter_context(nc.sbuf_tensor(name, shape, dt))

        def sem(name):
            return ctx.enter_context(nc.semaphore(name))

        bank = ctx.enter_context(nc.psum_tensor("bank", [P, 8, 512], F32))

        qk_parts = nc.dram_tensor("qk_parts", (2, 3, P, T), BF16, kind="Internal").ap()
        max_parts = nc.dram_tensor("max_parts", (NHG, 3, HG * NT, P), BF16, kind="Internal").ap()

        x = sb("x", [P, NT, C])
        kept = sb("kept", [P, NT, C])
        ident = sb("ident", [P, P])
        identb = sb("identb", [P, P], BF16)
        stat = sb("stat", [P, 6, NT])
        wqk = sb("wqk", [P, 2 * INNER])
        wv = sb("wv", [P, INNER])
        wo = sb("wo", [P, 8, C])
        w1 = sb("w1", [P, 2, 2 * FF])
        w2 = sb("w2", [P, 2, 3, C])
        b1 = sb("b1", [P, 2, 2 * FF])
        b2 = sb("b2", [P, 2, C])
        ln_g = sb("ln_g", [P, L])
        ln_b = sb("ln_b", [P, L])
        rot = sb("rot", [P, 4, DH])
        qks = sb("qks", [P, 2, L, DH])
        table = sb("table", [P, L, 2, 2, DH])
        back = sb("back", [P, P])
        centre = sb("centre", [P, P])
        mean = sb("mean", [P, P])
        pattern = sb("pattern", [P, 2 * W], BF16)
        pattern8 = sb("pattern8", [P, 8, 2 * W], BF16)
        select = sb("select", [P, NT, P], BF16)
        carry = sb("carry", [P, NT])

        arena = sb("arena", [P, 26880])
        used = [0]

        def part(*shape, dt=F32):
            size = int(np.prod(shape)) // (2 if dt == BF16 else 1)
            v = arena[:, used[0]:used[0] + size]
            used[0] += size
            assert used[0] <= 26880, used
            if dt != F32:
                v = v.bitcast(dt)
            if len(shape) == 1:
                return v
            names = "abcdef"[:len(shape)]
            return v.rearrange(f"p ({' '.join(names)}) -> p {' '.join(names)}",
                               **{n: d for n, d in zip(names[1:], shape[1:])})

        qst = part(2, HG, T, dt=BF16)
        kst = part(2, HG, T, dt=BF16)
        ring = part(8, QC)
        _ = part(QC, 4)
        used[0] -= 4 * QC
        o_sb = part(QC)
        vaug = part(NT, H1, D1 + 1)
        vcur = part(NT, HG, D1 + 1)
        pmax = part(HG * NT, 2)
        negm = part(P)
        mrest = part(P)
        mpart = part(3, P, dt=BF16)
        trik = part(QC, dt=BF16)
        triq = part(P, dt=BF16)
        rden = part(HG * NQC)
        xn = arena[:, 4096:6144].rearrange("p (t c) -> p t c", t=NT)
        xnT = arena[:, 6144:8192]
        raw = arena[:, 12288:14336]
        parts_q, parts_k = ([arena[:, o + 1024 * i:o + 1024 * (i + 1)].bitcast(BF16) for i in range(3)]
                            for o in (14336, 17408))
        z = arena[:, 0:2048].rearrange("p (t c) -> p t c", t=NT)
        zsq = arena[:, 2048:4096].rearrange("p (t c) -> p t c", t=NT)
        y1T = arena[:, 4096:6144]

        used[0] = 0
        xcur = part(P)
        xsT = part(W + P + 1)
        part(3)
        qkn = part(2, H, DH)
        rots = part(2, H, DH)
        sq = part(2 * H * DH)
        qT = part(8, P)
        kT = part(8, W + P)
        vv = part(2, WPT, 8, DH)
        prob = part(8, 2, 2 * W)
        probT = part(8, P)
        att = part(8, 2, DH)
        attT = part(8, P)
        ss = part(2 * H)
        rt = part(2 * H)
        rn = part(2 * H)
        fetch = part(1)
        eps = part(1)
        smax, ssum, rsum = part(H), part(H), part(H)
        xm = part(P)
        xmT = part(P + 2)
        xc, xcg, xsq, dev, rstd = (part(P) for _ in range(5))
        hg = part(2 * FF)
        gg = part(FF)
        gated = part(FF)
        hT = part(3, P)

        w_in = sb("w_in", [P, 4, C])
        b_qk = sb("b_qk", [P, 2])
        b_vo = sb("b_vo", [P, 2, C])

        all_done = sem("all_done")
        attT_read = sem("attT_read")
        attT_ready = sem("attT_ready")
        att_ready = sem("att_ready")
        back_read = sem("back_read")
        back_ready = sem("back_ready")
        carry_zero = sem("carry_zero")
        const_in = sem("const_in")
        cos_ready = sem("cos_ready")
        den_ready = sem("den_ready")
        dev_ready = sem("dev_ready")
        exp_done = sem("exp_done")
        gelu_ready = sem("gelu_ready")
        hT_read = sem("hT_read")
        hT_ready = sem("hT_ready")
        h_read = sem("h_read")
        h_ready = sem("h_ready")
        hh_ready = sem("hh_ready")
        ident_in = sem("ident_in")
        identb_ready = sem("identb_ready")
        ln_step = sem("ln_step")
        max_in = sem("max_in")
        max_out = sem("max_out")
        max_step = sem("max_step")
        mpart_ready = sem("mpart_ready")
        negmT_ready = sem("negmT_ready")
        negm_ready = sem("negm_ready")
        oT_read = sem("oT_read")
        oT_ready = sem("oT_ready")
        o_read = sem("o_read")
        ones_in = sem("ones_in")
        out_done = sem("out_done")
        pT_read = sem("pT_read")
        pT_ready = sem("pT_ready")
        parts_out = sem("parts_out")
        parts_ready = sem("parts_ready")
        pattern_ready = sem("pattern_ready")
        piece_read = sem("piece_read")
        piece_ready = sem("piece_ready")
        pv_done = sem("pv_done")
        pv_ready = sem("pv_ready")
        qkT_read = sem("qkT_read")
        qkT_ready = sem("qkT_ready")
        qk_proj = sem("qk_proj")
        qk_read = sem("qk_read")
        qk_ready = sem("qk_ready")
        qk_sq = sem("qk_sq")
        qkn_ready = sem("qkn_ready")
        rn_ready = sem("rn_ready")
        rot_ready = sem("rot_ready")
        rstd_ready = sem("rstd_ready")
        rt_ready = sem("rt_ready")
        s_exp = sem("s_exp")
        s_max = sem("s_max")
        s_ready = sem("s_ready")
        s_rsum = sem("s_rsum")
        s_sub = sem("s_sub")
        s_sum = sem("s_sum")
        score_ready = sem("score_ready")
        sin_ready = sem("sin_ready")
        sqrt_ready = sem("sqrt_ready")
        ss_ready = sem("ss_ready")
        ss_step = sem("ss_step")
        stack_clear = sem("stack_clear")
        stack_in = sem("stack_in")
        sumsq_ready = sem("sumsq_ready")
        v_proj = sem("v_proj")
        v_read = sem("v_read")
        v_ready = sem("v_ready")
        var_ready = sem("var_ready")
        vaug_ready = sem("vaug_ready")
        vcur_ready = sem("vcur_ready")
        vec_step = sem("vec_step")
        w2_ready = sem("w2_ready")
        w_in_in = sem("w_in_in")
        w_loaded = sem("w_loaded")
        wo_loaded = sem("wo_loaded")
        wo_ready = sem("wo_ready")
        wqk_loaded = sem("wqk_loaded")
        wv_loaded = sem("wv_loaded")
        xT_ready = sem("xT_ready")
        x_done = sem("x_done")
        x_in = sem("x_in")
        x_low = sem("x_low")
        x_step = sem("x_step")
        xb_ready = sem("xb_ready")
        xc_read = sem("xc_read")
        xc_ready = sem("xc_ready")
        xcur_ready = sem("xcur_ready")
        xmT_read = sem("xmT_read")
        xmT_ready = sem("xmT_ready")
        xm_ready = sem("xm_ready")
        xm_step = sem("xm_step")
        xnT_read = sem("xnT_read")
        xnT_ready = sem("xnT_ready")
        xn_ready = sem("xn_ready")
        xnf_ready = sem("xnf_ready")
        xs_ready = sem("xs_ready")
        xsq_ready = sem("xsq_ready")
        yT_read = sem("yT_read")
        yT_ready = sem("yT_ready")
        z_read = sem("z_read")
        z_ready = sem("z_ready")

        NW = 5
        NCONST = 13
        NSTACK = 19
        block = ctx.enter_context(nc.Block())

        def weights(sp, l, w):
            one = lambda n: a[n][bass.ds(l, 1)]
            slot = bass.ds(w, 1)
            for o, i in (
                (w1[:, slot], one("L0_ffn_W1").rearrange("l c n -> c l n")),
                (w2[:, slot, 0:2], one("L0_ffn_W2")[:, 0:2 * P].rearrange("l (k p) n -> p l k n", p=P)),
                (w2[0:FF - 2 * P, slot, 2], one("L0_ffn_W2")[:, 2 * P:FF].rearrange("l p n -> p l n")),
                (b1[:, slot], one("L0_ffn_b1").partition_broadcast(P)),
                (b2[:, slot], one("L0_ffn_b2").partition_broadcast(P)),
            ):
                sp.dma_start(o, i).then_inc(w_loaded, 16)

        def weights_qk(sp, l):
            sp.dma_start(wqk[:, :], a["L0_ffn_Wqkv"][bass.ds(l, 1), :, 0:2 * INNER].rearrange("l c n -> c (l n)")).then_inc(wqk_loaded, 16)

        def weights_v(sp, l):
            sp.dma_start(wv[:, :], a["L0_ffn_Wqkv"][bass.ds(l, 1), :, 2 * INNER:3 * INNER].rearrange("l c n -> c (l n)")).then_inc(wv_loaded, 16)

        def weights_o(sp, l):
            sp.dma_start(wo[:, :, :], a["L0_ffn_Wo"][bass.ds(l, 1)].rearrange("l (k p) n -> p (l k) n", p=P)).then_inc(wo_loaded, 16)

        def flat(eng, it):
            it(0, 0, True, False, False, False)
            it(1, 1, True, True, False, False)
            it(2, 0, True, True, True, False)
            it(3, 1, True, True, True, True)
            with eng.Fori(2, NTILE // 2 - 1) as m:
                it(2 * m, 0, True, True, True, True)
                it(2 * m + 1, 1, True, True, True, True)
            it(NTILE - 2, 0, True, True, True, True)
            it(NTILE - 1, 1, True, True, True, True)
            it(NTILE, 0, False, True, True, True)
            it(NTILE + 1, 1, False, False, True, True)
            it(NTILE + 2, 0, False, False, False, True)

        def tab(l, s, cs):
            return table[:, bass.ds(l, 1), s, cs, :]

        def first_query(qc, kt):
            return P * max(0, kt - QC // P * qc) if qc else 0

        @block.sync
        def _(sp):
            sp.dma_start(x[:, :, :], a["L0_attn_x"].rearrange("b (t p) c -> p (b t) c", p=P)).then_inc(x_in, 16)
            for i, n in enumerate("qkvo"):
                sp.dma_start(w_in[:, i, :], a[f"L0_attn_W{n}"]).then_inc(w_in_in, 16)
            for i, n in enumerate("qk"):
                sp.dma_start(b_qk[:, i:i + 1], a[f"L0_attn_b{n}"].rearrange("(p o) -> p o", o=1)).then_inc(w_in_in, 16)
            for i, n in enumerate("vo"):
                sp.dma_start(b_vo[:, i, :], a[f"L0_attn_b{n}"].partition_broadcast(P)).then_inc(w_in_in, 16)
            for s, p3 in ((0, parts_q), (1, parts_k)):
                for i in range(3):
                    sp.wait_ge(parts_ready, 3 * s + i + 1)
                    sp.dma_start(qk_parts[s, i], p3[i]).then_inc(parts_out, 16)
            sp.wait_ge(parts_out, 96)

            def stack(g, slot):
                for i in range(3):
                    for j in range(3):
                        r = (3 * i + j) * D1
                        for s, n, dst in ((0, i, qst), (1, j, kst)):
                            src = qk_parts[s, n].rearrange("(g h d) t -> d g h t", g=NHG, h=HG)[:, bass.ds(g, 1)]
                            sp.dma_start(dst[r:r + D1, bass.ds(slot, 1)], src).then_inc(stack_in, 16)
                sp.dma_start(qst[ROWS:ROWS + 3, bass.ds(slot, 1)],
                             a["c_zeros"].rearrange("r (s h t) -> r s h t", s=1, h=HG)).then_inc(stack_in, 16)

            def maxima(g, slot):
                sp.wait_ge(mpart_ready, g + 1)
                sp.dma_start(max_parts[bass.ds(g, 1)].rearrange("g i m q -> m (g i) q"),
                             mpart[0:HG * NT]).then_inc(max_out, 16)
                sp.wait_ge(max_out, 16 * (g + 1))
                sp.dma_start(qst[ROWS:ROWS + 3, bass.ds(slot, 1)],
                             max_parts[bass.ds(g, 1)].rearrange("g i (h t) q -> i g h (t q)", h=HG)).then_inc(max_in, 16)

            for s in range(2):
                sp.wait_ge(stack_clear, 2 * (s + 1))
                sp.dma_start(kst[ROWS:ROWS + 3, s], a["c_ones"].rearrange("r (h t) -> r h t", h=HG)).then_inc(ones_in, 16)
                stack(s, s)
                sp.wait_ge(ones_in, 16 * (s + 1))
                sp.wait_ge(stack_in, 16 * NSTACK * (s + 1))
            weights(sp, 0, 0)
            sp.wait_ge(w_loaded, 16 * NW)
            weights_qk(sp, 0)
            weights_v(sp, 0)
            weights_o(sp, 0)
            weights(sp, 1, 1)
            maxima(0, 0)
            with sp.Fori(1, NHG - 1) as g:
                maxima(g, g % 2)
                sp.wait_ge(pv_done, NS * g)
                stack(g + 1, (g + 1) % 2)
            maxima(NHG - 1, (NHG - 1) % 2)
            for l in range(1, L):
                sp.wait_ge(w_loaded, 16 * NW * (l + 1))
                sp.wait_ge(qk_proj, 2 * NT * l)
                weights_qk(sp, l)
                sp.wait_ge(v_proj, WPT * NT * l)
                weights_v(sp, l)
                sp.wait_ge(wo_ready, NT * l)
                weights_o(sp, l)
                if l + 1 < L:
                    sp.wait_ge(w2_ready, NT * l)
                    sp.wait_ge(x_done, NT * (l + 1))
                    weights(sp, l + 1, (l + 1) % 2)
            sp.wait_ge(all_done, 1)
            sp.dma_start(out.rearrange("b (t p) c -> p (b t) c", p=P), x[:, :, :]).then_inc(out_done, 16)
            sp.wait_ge(out_done, 16)

        @block.gpsimd
        def _(gp):
            gp.dma_start(ident[:, :], a["c_ident"]).then_inc(ident_in, 16)
            for dst, n in ((rot[:, :, :], "rot"), (back[:, :], "back"), (centre[:, :], "centre"), (mean[:, :], "mean"),
                           (pattern[:, :], "pattern"), (select[:, :, :], "select"), (carry[:, :], "carry"),
                           (trik, "tri_k"), (triq, "tri_q")):
                gp.dma_start(dst, a[f"c_{n}"]).then_inc(const_in, 16)
            with nc.allow_non_contiguous_dma(reason="a column a layer"):
                gp.dma_start(ln_g[:, :], a["L0_ffn_ln_g"].rearrange("l c -> c l")).then_inc(const_in, 16)
                gp.dma_start(ln_b[:, :], a["L0_ffn_ln_b"].rearrange("l c -> c l")).then_inc(const_in, 16)
            for i, n in enumerate(("q_scale", "k_scale")):
                gp.dma_start(qks[:, i], a[f"L0_ffn_{n}"].partition_broadcast(P)).then_inc(const_in, 16)

            gp.memset(arena[64:P, 0:4096], 0.0).then_inc(stack_clear, 1)
            gp.memset(arena[64:P, 8192:12288], 0.0).then_inc(stack_clear, 1)
            gp.wait_ge(parts_out, 96)
            gp.wait_ge(v_ready, 4)
            gp.memset(arena[64:P, 4096:8192], 0.0).then_inc(stack_clear, 1)
            gp.memset(arena[64:P, 12288:16384], 0.0).then_inc(stack_clear, 1)

            def it(n, parity, A, B, F, G):
                k = n - 2

                def sine_half(s):
                    gp.wait_ge(rot_ready, 2 * n)
                    gp.wait_ge(qkn_ready, 2 * n + s + 1)
                    for o, i in ((0, DH // 2), (DH // 2, 0)):
                        gp.tensor_tensor(rots[:, s, :, o:o + DH // 2], qkn[:, s, :, i:i + DH // 2],
                                         tab(n // NT, s, 1)[:, :, o:o + DH // 2].to_broadcast([P, H, DH // 2]),
                                         ALU.mult).then_inc(sin_ready, 1)

                if A:
                    sine_half(0)
                if G:
                    gp.wait_ge(hT_ready, k - 1)
                    gp.wait_ge(gelu_ready, k)
                    gp.tensor_tensor(gated[:, :], hg[:, 0:FF], gg[:, :], ALU.mult).then_inc(hh_ready, 1)
                if A:
                    sine_half(1)
                if B:
                    w, t = (n - 1) // NT % 2, bass.ds((n - 1) % NT, 1)
                    row = x[:, t, :].rearrange("p o c -> p (o c)")
                    gp.wait_ge(xm_ready, n)
                    gp.tensor_tensor(row, xm[:, :], b2[:, bass.ds(w, 1), :].rearrange("p o c -> p (o c)"), ALU.add).then_inc(xb_ready, 1)

            flat(gp, it)

        @block.scalar
        def _(act):
            def norm_sqrt(i):
                act.wait_ge(sumsq_ready, i + 1)
                act.activation(stat[:, 5, :], stat[:, 4, :], ACT.Sqrt).then_inc(sqrt_ready, 1)

            norm_sqrt(0)
            for b in range(4):
                act.wait_ge(xnT_ready, b + 1)
                act.activation(xnT[:, 512 * b:512 * b + 512], bank[:, b, :], ACT.Copy).then_inc(xnT_read, 1)
            act.wait_ge(w_in_in, 128)
            for s in range(2):
                if s:
                    act.wait_ge(parts_ready, 3)
                for b in range(4):
                    act.wait_ge(qk_ready, 4 * s + b + 1)
                    act.activation(raw[:, 512 * b:512 * b + 512], bank[:, (4 - 4 * s) + b, :], ACT.Identity,
                                   bias=b_qk[:, s:s + 1]).then_inc(qk_read, 1)

            def exps(k):
                for s, (qc, kt) in enumerate(steps):
                    lo = first_query(qc, kt)
                    for h in range(HG):
                        u = HG * s + h
                        act.wait_ge(score_ready, HG * NS * k + u + 1)
                        if h == 0:
                            act.wait_ge(pv_done, NS * k + (s - 1 if s >= 2 else 0))
                        act.activation(ring[:, u % 8, lo:QC], bank[:, 4 + u % 3, lo:QC], ACT.Exp,
                                       scale=SCALE1).then_inc(exp_done, 1)

            exps(0)
            with act.Fori(1, NHG) as k:
                exps(k)
            for b in range(4):
                act.wait_ge(yT_ready, b + 1)
                act.activation(y1T[:, 512 * b:512 * b + 512], bank[:, b, :], ACT.Copy).then_inc(yT_read, 1)
            norm_sqrt(1)
            norm_sqrt(2)

            def it(n, parity, A, B, F, G):
                k = n - 2

                def squares(half):
                    act.wait_ge(qk_proj, 2 * n + half + 1)
                    act.wait_ge(rot_ready, 2 * n)
                    act.activation(sq[:, H * DH * half:H * DH * (half + 1)],
                                   bank[:, 2 * half:2 * half + 2, :].rearrange("p b n -> p (b n)"), ACT.Square).then_inc(qk_sq, 1)

                def transposed_p(i):
                    act.wait_ge(pT_ready, 2 * (n - 1) + i + 1)
                    act.wait_ge(pv_ready, n - 1)
                    act.activation(probT[:, 4 * i:4 * i + 4, :], bank[:, 4 + i, :].rearrange("p (k t) -> p k t", k=4),
                                   ACT.Copy).then_inc(pT_read, 1)

                def values(j):
                    if B:
                        act.wait_ge(pv_ready, n - 1)
                    act.wait_ge(v_proj, 4 * n + j + 1)
                    act.activation(vv[:, parity, j], bank[:, 6 + j % 2, :].rearrange("p (k d) -> p k d", k=8),
                                   ACT.Copy).then_inc(v_read, 1)

                def turned(half):
                    for b in (2 * half, 2 * half + 1):
                        act.wait_ge(qkT_ready, 4 * n + b + 1)
                        dst = qT[:, 4 * b:4 * b + 4, :] if b < 2 else kT[:, 4 * b - 8:4 * b - 4, W:W + P]
                        act.activation(dst, bank[:, b, :].rearrange("p (k t) -> p k t", k=4), ACT.Copy).then_inc(qkT_read, 1)

                if A:
                    squares(0)
                if B:
                    act.wait_ge(s_sub, n)
                    act.activation(prob[:, :, :, :], prob[:, :, :, :], ACT.Exp).then_inc(s_exp, 1)
                if A:
                    act.activation(fetch[:, :], carry[:, 0:1], ACT.Sqrt)
                if F:
                    act.wait_ge(xc_read, k + 1)
                    act.wait_ge(var_ready, k)
                    act.activation(xsq[:, :], xc[:, :], ACT.Square).then_inc(xsq_ready, 1)
                if A:
                    squares(1)
                    act.wait_ge(back_ready, n + 1)
                    act.wait_ge(s_ready, n)
                    act.activation(kT[:, :, 0:W], bank[:, 6, 0:8 * W].rearrange("p (k t) -> p k t", k=8),
                                   ACT.Copy).then_inc(back_read, 1)
                if B:
                    transposed_p(0)
                    transposed_p(1)
                if A:
                    act.wait_ge(rn_ready, n)
                    act.wait_ge(ss_ready, n + 1)
                    act.activation(rt[:, :], ss[:, :], ACT.Sqrt).then_inc(rt_ready, 1)
                if F:
                    act.wait_ge(rstd_ready, k)
                    act.wait_ge(var_ready, k + 1)
                    act.activation(dev[:, :], bank[:, 7, 0:P], ACT.Sqrt, bias=eps[:, 0:1]).then_inc(dev_ready, 1)
                if A:
                    values(0)
                    values(1)
                if G:
                    act.wait_ge(hh_ready, k - 1)
                    act.wait_ge(h_read, k)
                    act.activation(gg[:, :], hg[:, FF:2 * FF], ACT.Gelu).then_inc(gelu_ready, 1)
                if A:
                    act.activation(fetch[:, :], carry[:, 0:1], ACT.Exp)
                    values(2)
                    values(3)
                if G:
                    act.wait_ge(hT_ready, k)
                    act.wait_ge(w2_ready, k - 1)
                    act.activation(hT[:, 0:2, :], bank[:, 6, 0:2 * P].rearrange("p (k t) -> p k t", k=2),
                                   ACT.Copy).then_inc(hT_read, 1)
                    act.activation(hT[0:FF - 2 * P, 2, :], bank[0:FF - 2 * P, 6, 2 * P:3 * P], ACT.Copy).then_inc(hT_read, 1)
                if A:
                    turned(0)
                if B:
                    for i in range(2):
                        act.wait_ge(attT_ready, 2 * (n - 1) + i + 1)
                        act.wait_ge(wo_ready, n - 1)
                        act.activation(attT[:, 4 * i:4 * i + 4, :], bank[:, 4 + i, :].rearrange("p (k t) -> p k t", k=4),
                                       ACT.Copy).then_inc(attT_read, 1)
                if A:
                    turned(1)

            flat(act, it)
            norm_sqrt(3)

        @block.tensor
        def _(pe):
            mm = pe.matmul
            pe.wait_ge(ident_in, 16)
            for t in range(NT):
                if t == 0:
                    pe.wait_ge(xn_ready, 1)
                last = pe.transpose(bank[:, t // 4, P * (t % 4):P * (t % 4) + P], xn[:, t, :], ident[:, :])
                if t % 4 == 3:
                    last.then_inc(xnT_ready, 1)
            pe.wait_ge(w_in_in, 128)
            for s in range(2):
                for b in range(4):
                    pe.wait_ge(xnT_read, b + 1)
                    mm(bank[:, 4 - 4 * s + b, :], w_in[:, s, :], xnT[:, 512 * b:512 * b + 512],
                       start=True, stop=True).then_inc(qk_ready, 1)
            for t in range(NT):
                pe.wait_ge(qk_read, t // 4 + 1)
                last = mm(bank[:, 4 + t // 4, P * (t % 4):P * (t % 4) + P], xnT[:, P * t:P * t + P], w_in[:, 2, :],
                          start=True, stop=True)
                if t % 4 == 3:
                    last.then_inc(v_ready, 1)

            def scores_for_max(k, slot, i):
                h, t, c = pieces[i]
                pe.wait_ge(piece_read, NPC * k + (i - 1 if i >= 2 else 0))
                if i == 0:
                    pe.wait_ge(mpart_ready, k)
                keys = P * (t + 1)
                lo, hi = 1024 * c, min(keys, 1024 * (c + 1))
                for j in range(lo, hi, 512):
                    n = min(512, hi - j)
                    b = 2 * (i % 2) + (j - lo) // 512
                    diagonal = j + n == keys
                    last = mm(bank[:, b, 0:n], qst[:, bass.ds(slot, 1), h, P * t:P * t + P],
                              kst[:, bass.ds(slot, 1), h, j:j + n], start=True, stop=True)
                    if diagonal:
                        last = mm(bank[:, b, n - P:n], identb[:, :], triq, start=False, stop=True, skip_group_check=True)
                last.then_inc(piece_ready, 1)

            def turn_maxima(k):
                pe.wait_ge(negm_ready, k + 1)
                pe.transpose(bank[:, 0, 0:P], negm, ident[:, :]).then_inc(negmT_ready, 1)

            def scores(k, slot, s, h):
                qc, kt = steps[s]
                lo = first_query(qc, kt)
                if (s, h) == (0, 0):
                    pe.wait_ge(max_in, 16 * (k + 1))
                u = HG * s + h
                b = 4 + u % 3
                pe.wait_ge(exp_done, HG * NS * k + (u - 2 if u >= 3 else 0))
                r = kt - QC // P * qc
                last = mm(bank[:, b, lo:QC], kst[:, bass.ds(slot, 1), h, P * kt:P * kt + P],
                          qst[:, bass.ds(slot, 1), h, QC * qc + lo:QC * qc + QC], start=True, stop=True)
                if r >= 0:
                    hi = P * (r + 1)
                    last = mm(bank[:, b, lo:hi], identb[:, :], trik[:, QC - hi + lo:QC], start=False, stop=True,
                              skip_group_check=True)
                last.then_inc(score_ready, 1)

            def values(k, s):
                qc, kt = steps[s]
                lo = first_query(qc, kt)
                pe.wait_ge(exp_done, HG * NS * k + HG * (s + 1))
                if s == 0:
                    pe.wait_ge(vcur_ready, k + 1)
                if kt == 0:
                    pe.wait_ge(oT_read, NQC * k + qc)
                for h in range(HG):
                    last = mm(bank[32 * h:32 * h + D1 + 1, 7, lo:QC], vcur[:, kt, h, :], ring[:, (HG * s + h) % 8, lo:QC],
                              start=kt == 0, stop=True, skip_group_check=True)
                last.then_inc(pv_done, 1)

            def turn_output(k, qc):
                pe.wait_ge(o_read, NQC * k + qc + 1)
                for i in range(4):
                    last = pe.transpose(bank[:, 7, P * i:P * i + P], o_sb[:, P * i:P * i + P], ident[:, :])
                last.then_inc(oT_ready, 1)

            def group(k, slot, other, more):
                for what, *i in order:
                    if what == "score":
                        scores(k, slot, *i)
                    elif what == "pv":
                        values(k, i[0])
                    elif what == "out":
                        turn_output(k, i[0])
                    elif what == "max" and more:
                        if i[0] == 0:
                            if isinstance(k, int):
                                pe.wait_ge(ones_in, 32)
                            pe.wait_ge(stack_in, 16 * NSTACK * (k + 2))
                        scores_for_max(k + 1, other, i[0])
                    elif what == "split" and more:
                        turn_maxima(k + 1)

            pe.wait_ge(identb_ready, 1)
            pe.wait_ge(vaug_ready, 5)
            pe.wait_ge(const_in, 16 * NCONST)
            pe.wait_ge(ones_in, 16)
            pe.wait_ge(stack_in, 16 * NSTACK)
            for i in range(NPC):
                scores_for_max(0, 0, i)
            turn_maxima(0)
            group(0, 0, 1, True)
            with pe.Fori(1, NHG - 1) as k:
                group(k, k % 2, (k + 1) % 2, True)
            group(NHG - 1, (NHG - 1) % 2, NHG % 2, False)

            pe.wait_ge(oT_read, NHG * NQC)
            for t in range(NT):
                last = pe.transpose(bank[:, t // 4, P * (t % 4):P * (t % 4) + P], kept[:, t, :], ident[:, :])
                if t % 4 == 3:
                    last.then_inc(yT_ready, 1)
            for t in range(NT):
                pe.wait_ge(yT_read, t // 4 + 1)
                last = mm(bank[:, 4 + t // 4, P * (t % 4):P * (t % 4) + P], y1T[:, P * t:P * t + P], w_in[:, 3, :],
                          start=True, stop=True)
                if t % 4 == 3:
                    last.then_inc(z_ready, 1)

            def it(n, parity, A, B, F, G):
                wg = (n - 3) // NT % 2 if G else None
                k = n - 2

                def turn_tile():
                    pe.wait_ge(xm_ready, n)
                    pe.transpose(bank[:, 0, P:2 * P], xm[:, :], ident[:, :]).then_inc(xmT_ready, 1)

                def project(half):
                    for b in (2 * half, 2 * half + 1):
                        last = mm(bank[:, b, :], xsT[:, W:W + P],
                                  wqk[:, 512 * b:512 * b + 512], start=True, stop=True)
                    last.then_inc(qk_proj, 1)

                def turn_qk(half):
                    pe.wait_ge(rot_ready, 2 * n + half + 1)
                    for i in range(8 * half, 8 * half + 8):
                        src = qkn[:, i // 8, 2 * (i % 8):2 * (i % 8) + 2, :].rearrange("p h d -> p (h d)")
                        last = pe.transpose(bank[:, i // 4, P * (i % 4):P * (i % 4) + P], src, ident[:, :])
                        if i % 4 == 3:
                            last.then_inc(qkT_ready, 1)

                def value_projection(j):
                    wv2 = wv[:, :].rearrange("p (k h d) -> p k h d", h=2, d=DH)
                    if j == 0:
                        pe.wait_ge(wv_loaded, 16 * (n // NT + 1))
                        pe.wait_ge(back_read, n + 1)
                    elif j == 1 and F:
                        pe.wait_ge(dev_ready, k + 1)
                    elif j >= 2:
                        pe.wait_ge(v_read, 4 * n + j - 1)
                    for odd in range(2):
                        if j == 1 and odd == 1 and B:
                            pe.wait_ge(pT_read, 2 * n)
                        last = mm(bank[DH * odd:DH * odd + DH, 6 + j % 2, :], xsT[:, W * j:W * j + 2 * W], wv2[:, :, odd, :],
                                  start=True, stop=True)
                    last.then_inc(v_proj, 1)

                def project_output(half):
                    if not half:
                        pe.wait_ge(wo_loaded, 16 * ((n - 1) // NT + 1))
                    pe.wait_ge(attT_read, 2 * (n - 1) + half + 1)
                    for i in range(4 * half, 4 * half + 4):
                        last = mm(bank[:, 0, 0:P], attT[:, i, :], wo[:, i, :], start=i == 0, stop=i == 7,
                                  skip_group_check=True)
                    if half:
                        last.then_inc(wo_ready, 1)

                if F:
                    pe.wait_ge(xmT_read, k + 1)
                if A:
                    pe.wait_ge(xs_ready, n + 1)
                    project(0)
                if F:
                    if B:
                        pe.wait_ge(v_read, 4 * n)
                    if not isinstance(n, int) or n > 3:
                        pe.wait_ge(x_done, NT - 3 + n)
                    mm(bank[:, 6, 3 * P:4 * P], centre[:, :], xmT[:, 0:P], start=True, stop=True).then_inc(xc_ready, 1)
                if G:
                    pe.wait_ge(xnf_ready, k)
                    if not F:
                        pe.wait_ge(x_done, NT - 3 + n)
                    for i in range(2):
                        last = mm(bank[:, 6 + i, 0:FF], xcg[:, :], w1[:, bass.ds(wg, 1), FF * i:FF * i + FF],
                                  start=True, stop=True)
                    last.then_inc(h_ready, 1)
                if A:
                    project(1)
                if B:
                    pe.wait_ge(s_exp, n)
                    for i in range(8):
                        last = pe.transpose(bank[:, 4 + i // 4, P * (i % 4):P * (i % 4) + P],
                                            prob[:, i].rearrange("p h c -> p (h c)"), ident[:, :])
                        if i % 4 == 3:
                            last.then_inc(pT_ready, 1)
                if A:
                    if F:
                        pe.wait_ge(xc_read, k + 1)
                    elif n == 0:
                        pe.wait_ge(carry_zero, 1)
                    else:
                        pe.wait_ge(v_read, 4 * n)
                    if G:
                        pe.wait_ge(h_read, k)
                    mm(bank[:, 6, 0:8 * W], back[:, :], kT[:, :, P:P + W], start=True, stop=True).then_inc(back_ready, 1)
                if F:
                    pe.wait_ge(xsq_ready, k + 1)
                    if G:
                        pe.wait_ge(h_read, k)
                    mm(bank[:, 7, 0:P], mean[:, :], xsq[:, :], start=True, stop=True).then_inc(var_ready, 1)
                if A:
                    value_projection(0)
                    value_projection(1)
                elif B:
                    pe.wait_ge(pT_read, 2 * n)
                if B:
                    for i in range(8):
                        for j in range(WPT):
                            for odd in range(2):
                                r = DH * odd
                                last = mm(bank[W * j:W * j + W, 4 + odd, DH * i:DH * i + DH], probT[r:r + DH, i, W * j:W * j + W],
                                          vv[r:r + DH, 1 - parity, j, i, :], start=True, stop=True)
                    last.then_inc(pv_ready, 1)
                if A:
                    value_projection(2)
                    value_projection(3)
                if G:
                    pe.wait_ge(hh_ready, k)
                    if A:
                        pe.wait_ge(v_read, 4 * n + 3)
                    elif F:
                        pe.wait_ge(xc_read, k + 1)
                    for i in range(3):
                        m = min(P, FF - P * i)
                        last = pe.transpose(bank[0:m, 6, P * i:P * i + P], gated[:, P * i:P * i + m], ident[:, :])
                    last.then_inc(hT_ready, 1)
                if A:
                    turn_qk(0)
                if B:
                    pe.wait_ge(att_ready, n)
                    for i in range(8):
                        last = pe.transpose(bank[:, 4 + i // 4, P * (i % 4):P * (i % 4) + P],
                                            att[:, i].rearrange("p h d -> p (h d)"), ident[:, :])
                        if i % 4 == 3:
                            last.then_inc(attT_ready, 1)
                if G:
                    pe.wait_ge(hT_read, 2 * k)
                    for i in range(3):
                        m = min(P, FF - P * i)
                        last = mm(bank[:, 6, 3 * P:4 * P], hT[0:m, i, :], w2[0:m, bass.ds(wg, 1), i, :], start=i == 0, stop=i == 2)
                    last.then_inc(w2_ready, 1)
                if B:
                    if A:
                        pe.wait_ge(qkT_read, 4 * n + 1)
                    project_output(0)
                if A:
                    turn_qk(1)
                    pe.wait_ge(xcur_ready, n + 2)
                    pe.wait_ge(qkT_read, 4 * n + 2)
                    pe.transpose(bank[:, 1, 0:P], xcur[:, :], ident[:, :]).then_inc(xT_ready, 1)
                if B:
                    project_output(1)
                if A:
                    if B:
                        pe.wait_ge(attT_read, 2 * n)
                    pe.wait_ge(back_read, n + 1)
                    pe.wait_ge(qkT_read, 4 * n + 4)
                    if isinstance(n, int) and n == 0:
                        pe.wait_ge(pattern_ready, 1)
                    for odd in range(2):
                        mm(bank[:, 4 + odd, :], select[:, bass.ds(n % NT, 1), :], pattern8[:, :, :], start=True, stop=True)
                    for i in range(8):
                        if i == 4 and B:
                            turn_tile()
                        for j in range(WPT):
                            for odd in range(2):
                                r = DH * odd
                                last = mm(bank[W * j:W * j + W, 4 + odd, 2 * W * i:2 * W * i + 2 * W],
                                          qT[r:r + DH, i, W * j:W * j + W], kT[r:r + DH, i, W * j:W * j + 2 * W],
                                          start=False, stop=True, skip_group_check=True)
                    last.then_inc(s_ready, 1)
                elif B:
                    turn_tile()
            pe.wait_ge(xcur_ready, 1)
            pe.wait_ge(z_read, 4)
            pe.transpose(bank[:, 1, 0:P], xcur[:, :], ident[:, :]).then_inc(xT_ready, 1)
            flat(pe, it)

        @block.vector
        def _(ve):
            count = [0]

            def step(ins):
                count[0] += 1
                ins.then_inc(vec_step, 1)
                ve.wait_ge(vec_step, count[0])

            def over(s, n):
                return stat[:, s, :].unsqueeze(2).to_broadcast([P, NT, n])

            def norm(i, src, dst, work):
                step(ve.tensor_reduce(stat[:, 0, :], src, AX.X, ALU.add))
                step(ve.tensor_scalar(stat[:, 1, :], stat[:, 0, :], -1.0 / C, None, ALU.mult))
                step(ve.tensor_tensor(dst, src, over(1, C), ALU.add))
                step(ve.tensor_tensor(work, dst, dst, ALU.mult))
                step(ve.tensor_reduce(stat[:, 3, :], work, AX.X, ALU.add))
                ve.tensor_scalar(stat[:, 4, :], stat[:, 3, :], 1.0 / C, EPS, ALU.mult, ALU.add).then_inc(sumsq_ready, 1)
                ve.wait_ge(sqrt_ready, i + 1)
                step(ve.reciprocal(stat[:, 4, :], stat[:, 5, :]))

            ve.wait_ge(x_in, 16)
            norm(0, x[:, :, :], xn, raw.rearrange("p (t c) -> p t c", t=NT))
            ve.tensor_tensor(xn, xn, over(4, C), ALU.mult).then_inc(xn_ready, 1)
            ve.wait_ge(ident_in, 16)
            ve.tensor_copy(identb[:, :], ident[:, :]).then_inc(identb_ready, 1)
            step(ve.memset(vaug[:, :, :, D1:D1 + 1], 1.0))
            step(ve.memset(pmax, NEG))
            step(ve.memset(negm, 0.0))
            ve.wait_ge(const_in, 16 * NCONST)
            half = DH // 2
            for s in range(2):
                for cs, o, i, m in ((0, 0, 0, DH), (1, 0, half, half), (1, half, 0, half)):
                    step(ve.tensor_tensor(table[:, :, s, cs, o:o + m], qks[:, s, :, i:i + m],
                                          rot[:, 2 * s + cs:2 * s + cs + 1, o:o + m].to_broadcast([P, L, m]), ALU.mult))
            ve.tensor_copy(pattern8[:, :, :], pattern[:, :].unsqueeze(1).to_broadcast([P, 8, 2 * W])).then_inc(pattern_ready, 1)
            for s, p3 in ((0, parts_q), (1, parts_k)):
                ve.wait_ge(qk_read, 4 * (s + 1))
                for i in range(3):
                    ve.tensor_copy(p3[i], raw).then_inc(parts_ready, 1)
                    if i < 2:
                        ve.wait_ge(parts_ready, 3 * s + i + 1)
                        step(ve.tensor_tensor(raw, raw, p3[i], ALU.subtract))
            ve.wait_ge(w_in_in, 128)
            for b in range(4):
                ve.wait_ge(v_ready, b + 1)
                bias = b_vo[:, 0:1, :].rearrange("p o (h d) -> p o h d", h=H1).to_broadcast([P, 4, H1, D1])
                ve.tensor_tensor(vaug[:, 4 * b:4 * b + 4, :, 0:D1],
                                 bank[:, 4 + b, :].rearrange("p (t h d) -> p t h d", t=4, h=H1), bias, ALU.add).then_inc(vaug_ready, 1)
            ve.wait_ge(vaug_ready, 4)
            ve.memset(bank[:, 7, :], 0.0).then_inc(vaug_ready, 1)
            ve.wait_ge(vaug_ready, 5)

            def max_piece(k, i):
                h, t, c = pieces[i]
                n = min(P * (t + 1) - 1024 * c, 1024)
                ve.wait_ge(piece_ready, NPC * k + i + 1)
                src = bank[:, 2 * (i % 2):2 * (i % 2) + 2, :].rearrange("p b n -> p (b n)")[:, 0:n]
                ve.tensor_reduce(pmax[:, h * NT + t, c:c + 1], src, AX.X, ALU.max).then_inc(piece_read, 1)

            def split_maxima(k):
                ve.wait_ge(piece_read, NPC * (k + 1))
                m = negm[:, 0:HG * NT]
                ve.tensor_reduce(m, pmax, AX.X, ALU.max).then_inc(max_step, 1)
                ve.wait_ge(max_step, 5 * k + 1)
                ve.tensor_scalar(m, m, -1.0, None, ALU.mult).then_inc(negm_ready, 1)
                ve.wait_ge(negmT_ready, k + 1)
                ve.wait_ge(max_out, 16 * k)
                ve.tensor_copy(mpart[:, 0, :], bank[:, 0, 0:P]).then_inc(max_step, 1)
                ve.wait_ge(max_step, 5 * k + 2)
                ve.tensor_tensor(mrest, bank[:, 0, 0:P], mpart[:, 0, :], ALU.subtract).then_inc(max_step, 1)
                ve.wait_ge(max_step, 5 * k + 3)
                ve.tensor_copy(mpart[:, 1, :], mrest).then_inc(max_step, 1)
                ve.wait_ge(max_step, 5 * k + 4)
                ve.tensor_tensor(mrest, mrest, mpart[:, 1, :], ALU.subtract).then_inc(max_step, 1)
                ve.wait_ge(max_step, 5 * k + 5)
                ve.tensor_copy(mpart[:, 2, :], mrest).then_inc(mpart_ready, 1)

            y = kept[:, :, :].rearrange("p t (g h d) -> p t g h d", g=NHG, h=HG)

            def group(k, more):
                ve.wait_ge(pv_done, NS * k)
                ve.tensor_copy(vcur, vaug[:, :, bass.ds(HG * k, HG), :]).then_inc(vcur_ready, 1)
                for what, *i in order:
                    if what == "pv":
                        qc, kt = steps[i[0]]
                        if kt == QC // P * (qc + 1) - 1:
                            ve.wait_ge(pv_done, NS * k + i[0] + 1)
                            ve.wait_ge(oT_ready, NQC * k + qc)
                            ve.tensor_copy(o_sb, bank[:, 7, :]).then_inc(o_read, 1)
                    elif what == "out":
                        qc = i[0]
                        o = bank[:, 7, :].rearrange("p (t h d) -> p t h d", t=4, h=HG)
                        r = rden.rearrange("p (t h o) -> p t h o", t=4, h=HG)
                        ve.wait_ge(oT_ready, NQC * k + qc + 1)
                        ve.wait_ge(oT_read, NQC * k + qc)
                        ve.reciprocal(r, o[:, :, :, D1:D1 + 1]).then_inc(den_ready, 1)
                        ve.wait_ge(den_ready, NQC * k + qc + 1)
                        dst = y[:, 4 * qc:4 * qc + 4, bass.ds(k, 1), :, :].rearrange("p t g h d -> p t (g h) d")
                        ve.tensor_tensor(dst, o[:, :, :, 0:D1], r.to_broadcast([P, 4, HG, D1]), ALU.mult).then_inc(oT_read, 1)
                    elif what == "max" and more:
                        max_piece(k + 1, i[0])
                    elif what == "split" and more:
                        split_maxima(k + 1)

            for i in range(NPC):
                max_piece(0, i)
            split_maxima(0)
            group(0, True)
            with ve.Fori(1, NHG - 1) as k:
                group(k, True)
            group(NHG - 1, False)

            for b in range(4):
                ve.wait_ge(z_ready, b + 1)
                ve.tensor_tensor(z[:, 4 * b:4 * b + 4, :], bank[:, 4 + b, :].rearrange("p (t c) -> p t c", t=4),
                                 b_vo[:, 1:2, :].to_broadcast([P, 4, C]), ALU.add).then_inc(z_read, 1)
            ve.wait_ge(z_read, 4)
            norm(1, z, z, zsq)
            step(ve.tensor_tensor(z, z, over(4, C), ALU.mult))
            step(ve.tensor_tensor(kept[:, :, :], x[:, :, :], z, ALU.add))
            norm(2, kept[:, :, :], x[:, :, :], zsq)
            for t in range(NT):
                ve.tensor_scalar(x[:, t, :], x[:, t, :], stat[:, 4, t:t + 1], None, ALU.mult).then_inc(x_done, 1)

            ve.wait_ge(x_done, NT)
            step(ve.memset(kT, 0.0))
            step(ve.memset(xsT, 0.0))
            step(ve.memset(xmT, 0.0))
            step(ve.memset(eps, EPS))
            ve.memset(gated[:, :], 0.0).then_inc(carry_zero, 1)
            ve.wait_ge(carry_zero, 1)

            def x_copy(n):
                ve.wait_ge(x_done, n + 1)
                ve.wait_ge(xT_ready, n)
                ve.tensor_copy(xcur[:, :], x[:, bass.ds(n % NT, 1), :].rearrange("p o c -> p (o c)")).then_inc(xcur_ready, 1)

            def shift_window(n):
                if not isinstance(n, int) or n > 0:
                    ve.wait_ge(v_proj, 4 * n)
                ve.tensor_scalar(xsT[:, 0:W + 1], xsT[:, P:P + W + 1], carry[:, bass.ds(n % NT, 1)], None,
                                 ALU.mult).then_inc(x_step, 1)

            def shift_low(n):
                ve.wait_ge(x_step, n + 1)
                ve.wait_ge(xT_ready, n + 1)
                ve.tensor_copy(xsT[0:64, W:W + P], bank[0:64, 1, 0:P]).then_inc(x_low, 1)

            def shift_high(n):
                if not isinstance(n, int) or n < NTILE:
                    ve.wait_ge(wqk_loaded, 16 * (n // NT + 1))
                ve.wait_ge(x_low, n + 1)
                ve.tensor_copy(xsT[64:P, W + 1:W + P + 1], bank[64:P, 1, 0:P]).then_inc(xs_ready, 1)

            def it(n, parity, A, B, F, G):
                wg = (n - 3) // NT % 2 if G else None
                k = n - 2
                tb, tg = (bass.ds((n - d) % NT, 1) if on else None for d, on in ((1, B), (3, G)))
                flatten = lambda v: v.rearrange("p o c -> p (o c)")
                p4 = prob.rearrange("p k h c -> p h k c")
                by_head = lambda v: v.rearrange("p (h k) -> p h k", h=2)
                sq4 = sq.rearrange("p (s h d) -> p s h d", s=2, h=H)

                def sum_squares(s):
                    ve.wait_ge(qk_sq, 2 * n + s + 1)
                    ve.wait_ge(rt_ready, n)
                    ve.tensor_reduce(ss[:, H * s:H * s + H], sq4[:, s], AX.X, ALU.add).then_inc(ss_step, 1)

                def normalised(s):
                    ve.tensor_tensor(qkn[:, s], bank[:, 2 * s:2 * s + 2, :].rearrange("p b (h d) -> p (b h) d", d=DH),
                                     rn[:, H * s:H * s + H].unsqueeze(2).to_broadcast([P, H, DH]), ALU.mult).then_inc(qkn_ready, 1)

                def cosine_half(s):
                    ve.wait_ge(qkn_ready, 2 * n + s + 1)
                    ve.tensor_tensor(sq4[:, s], qkn[:, s], tab(n // NT, s, 0).to_broadcast([P, H, DH]), ALU.mult).then_inc(cos_ready, 1)

                def rotated(s):
                    ve.wait_ge(cos_ready, 2 * n + s + 1)
                    ve.wait_ge(sin_ready, 4 * n + 2 * (s + 1))
                    ve.tensor_tensor(qkn[:, s], sq4[:, s], rots[:, s], ALU.add).then_inc(rot_ready, 1)

                if A:
                    sum_squares(0)
                if F:
                    ve.wait_ge(xc_ready, k + 1)
                    if G:
                        ve.wait_ge(h_ready, k)
                    ve.wait_ge(xnf_ready, k)
                    ve.wait_ge(xsq_ready, k)
                    ve.tensor_copy(xc[:, :], bank[:, 6, 3 * P:4 * P]).then_inc(xc_read, 1)
                if G:
                    ve.wait_ge(h_ready, k)
                    ve.wait_ge(hh_ready, k - 1)
                    ve.tensor_tensor(hg.rearrange("p (i f) -> p i f", i=2), bank[:, 6:8, 0:FF],
                                     b1[:, bass.ds(wg, 1), :].rearrange("p o (i f) -> p (o i) f", i=2), ALU.add).then_inc(h_read, 1)
                if A:
                    x_copy(n + 1)
                if B:
                    ve.wait_ge(s_exp, n)
                    ve.tensor_reduce(by_head(ssum), p4, AX.X, ALU.add).then_inc(s_sum, 1)
                if A:
                    sum_squares(1)
                if B:
                    ve.wait_ge(s_sum, n)
                    ve.wait_ge(att_ready, n - 1)
                    ve.reciprocal(rsum[:, :], ssum[:, :]).then_inc(s_rsum, 1)
                if A:
                    ve.wait_ge(ss_step, 2 * (n + 1))
                    ve.tensor_scalar(ss[:, :], ss[:, :], 1e-24, None, ALU.max).then_inc(ss_ready, 1)
                    ve.wait_ge(rt_ready, n + 1)
                    ve.wait_ge(qkn_ready, 2 * n)
                    ve.reciprocal(rn[:, :], rt[:, :]).then_inc(rn_ready, 1)
                    ve.wait_ge(rn_ready, n + 1)
                    ve.wait_ge(qkT_ready, 4 * n)
                    normalised(0)
                    cosine_half(0)
                    normalised(1)
                    rotated(0)
                if B:
                    ve.wait_ge(pv_ready, n)
                    ve.wait_ge(s_rsum, n)
                    ve.wait_ge(attT_ready, 2 * (n - 1))
                    ve.tensor_tensor(att.rearrange("p k h d -> p h k d"), bank[:, 4:6, :].rearrange("p b (k d) -> p b k d", d=DH),
                                     by_head(rsum).unsqueeze(3).to_broadcast([P, 2, 8, DH]), ALU.mult).then_inc(att_ready, 1)
                if A:
                    cosine_half(1)
                    rotated(1)
                if F:
                    ve.wait_ge(dev_ready, k + 1)
                    ve.wait_ge(xnf_ready, k)
                    ve.reciprocal(rstd[:, :], dev[:, :]).then_inc(rstd_ready, 1)
                if A:
                    shift_window(n + 1)
                if F:
                    ve.wait_ge(rstd_ready, k + 1)
                    ve.wait_ge(h_ready, k)
                    ln = bass.ds(k // NT, 1)
                    ve.scalar_tensor_tensor(out=xcg[:, :], in0=xc[:, :], scalar=ln_g[:, ln], in1=rstd[:, :], op0=ALU.mult,
                                            op1=ALU.mult).then_inc(ln_step, 1)
                if A:
                    shift_low(n + 1)
                if F:
                    ve.wait_ge(ln_step, k + 1)
                    ve.tensor_scalar(xcg[:, :], xcg[:, :], ln_b[:, ln], None, ALU.add).then_inc(xnf_ready, 1)
                if A:
                    shift_high(n + 1)
                if B:
                    ve.wait_ge(wo_ready, n)
                    ve.wait_ge(xmT_ready, n - 1)
                    ve.wait_ge(xb_ready, n - 1)
                    ve.tensor_tensor(xm[:, :], bank[:, 0, 0:P], flatten(x[:, tb, :]), ALU.add).then_inc(xm_ready, 1)
                    ve.wait_ge(xc_ready, n - 1)
                    ve.tensor_scalar(xmT[64:P, 0:1], xmT[64:P, P:P + 1], carry[64:P, tb], None, ALU.mult).then_inc(xm_step, 1)
                    ve.wait_ge(xmT_ready, n)
                    ve.tensor_copy(xmT[0:64, 0:P], bank[0:64, 0, P:2 * P]).then_inc(xm_step, 1)
                    ve.wait_ge(xm_step, 2 * n)
                    ve.tensor_copy(xmT[64:P, 1:P + 1], bank[64:P, 0, P:2 * P]).then_inc(xmT_read, 1)
                if G:
                    ve.wait_ge(w2_ready, k)
                    ve.wait_ge(xb_ready, k)
                    ve.tensor_tensor(flatten(x[:, tg, :]), bank[:, 6, 3 * P:4 * P], flatten(x[:, tg, :]), ALU.add).then_inc(x_done, 1)
                if A:
                    ve.wait_ge(s_ready, n + 1)
                    s4 = bank[:, 4:6, :].rearrange("p b (k c) -> p b k c", c=2 * W)
                    if B:
                        ve.wait_ge(s_sub, n)
                    ve.tensor_reduce(by_head(smax), s4, AX.X, ALU.max).then_inc(s_max, 1)
                    ve.wait_ge(s_max, n + 1)
                    ve.wait_ge(pT_ready, 2 * n)
                    ve.wait_ge(s_sum, n)
                    ve.tensor_tensor(p4, s4, by_head(smax).unsqueeze(3).to_broadcast([P, 2, 8, 2 * W]), ALU.subtract).then_inc(s_sub, 1)

            x_copy(0)
            shift_window(0)
            shift_low(0)
            shift_high(0)
            flat(ve, it)

            ve.wait_ge(x_done, NT + NTILE)
            ve.wait_ge(xs_ready, NTILE + 1)
            norm(3, x[:, :, :], z, zsq)
            step(ve.tensor_tensor(z, z, over(4, C), ALU.mult))
            ve.tensor_tensor(x[:, :, :], kept[:, :, :], z, ALU.add).then_inc(all_done, 1)


_INS = ["L0_attn_x"] + [f"L0_attn_{k}{n}" for n in "qkvo" for k in "Wb"] + [
    f"L0_ffn_{n}" for n in ("Wqkv", "q_scale", "k_scale", "Wo", "ln_g", "ln_b", "W1", "b1", "W2", "b2")]


def kernel(**inputs):
    import concourse.bacc as bacc
    from concourse.bass_utils import run_bass_kernel_spmd

    nc = bacc.Bacc("TRN2", target_bir_lowering=False, num_devices=1)
    arrays, aps = {}, {}
    data = {n: np.ascontiguousarray(inputs[n]) for n in _INS} | constants()
    for name, v in data.items():
        arrays[f"in_{name}"] = v
        aps[name] = nc.dram_tensor(f"in_{name}", v.shape, mybir.dt.from_np(v.dtype), kind="ExternalInput").ap()
        if v.dtype == np.uint16:
            aps[name] = aps[name].bitcast(BF16)
    out = nc.dram_tensor("out_0", (1, T, C), F32, kind="ExternalOutput").ap()
    build(nc, aps, out)
    r = run_bass_kernel_spmd(nc, [arrays], core_ids=[0])
    return r.results[0]["out_0"]
```
